# Optimizing a Trainium2 kernel written in Bass

```python
import numpy as np
import jax
import jax.numpy as jnp

def _softmax(x, axis=-1):
    return jax.nn.softmax(x, axis=axis)

def _gelu(x):
    return jax.nn.gelu(x, approximate=True)

def _silu(x):
    return jax.nn.silu(x)

def _sigmoid(x):
    return jax.nn.sigmoid(x)

def _layernorm(x, axis=-1, eps=1e-05):
    m = jnp.mean(x, axis=axis, keepdims=True)
    v = jnp.var(x, axis=axis, keepdims=True)
    return (x - m) / jnp.sqrt(v + eps)

def _scatter_add(tgt, idx, src, axis=0):
    return tgt.at[idx].add(src)

def _segment_sum(src, seg, n):
    return jax.ops.segment_sum(src, seg, n)
kernel_name = 'mk_gnn_preln_d2_gnn_r64_eb4a26'

def setup_inputs(seed: int=0):
    np.random.seed(seed)
    _w = jnp.asarray

    def _rec_inputs():
        import jax
        import jax.numpy as jnp
        _gk = jax.random.key(seed)
        x = -0.0003713 + 1 * jax.random.normal(jax.random.fold_in(_gk, 1), (100000, 128), jnp.float32)
        src = jax.random.randint(jax.random.fold_in(_gk, 2), (25000,), 0, 100000, jnp.int32)
        dst = jax.random.randint(jax.random.fold_in(_gk, 3), (25000,), 0, 100000, jnp.int32)
        _o = jnp.argsort(dst, stable=True)
        src = src[_o]
        dst = dst[_o]
        edge_attr_128 = -8.16379e-05 + 0.999858 * jax.random.normal(jax.random.fold_in(_gk, 12), (25000, 128), jnp.float32)
        edge_weight = jax.random.uniform(jax.random.fold_in(_gk, 14), (25000,), jnp.float32, 0.0, 0.999998)
        return (x, src, dst, edge_attr_128, edge_weight)
    x, src, dst, edge_attr_128, edge_weight = _rec_inputs()

    def _L0_gnn_setup():
        import jax, jax.numpy as jnp
        import numpy as np
        N_NODES = 100000
        D = 128

        def gcn_conv(x, W, b, src, dst, deg_inv_sqrt):
            h = x @ W
            norm = deg_inv_sqrt[src] * deg_inv_sqrt[dst]
            msgs = h[src] * norm[:, None]
            out = jax.ops.segment_sum(msgs, dst, num_segments=x.shape[0])
            return out + b

        def _prep_edges(edge_index, n_nodes):
            loops = jnp.arange(n_nodes, dtype=edge_index.dtype)
            src = jnp.concatenate([edge_index[0], loops])
            dst = jnp.concatenate([edge_index[1], loops])
            deg = jax.ops.segment_sum(jnp.ones_like(dst, dtype=jnp.float32), dst, num_segments=n_nodes)
            deg_inv_sqrt = jnp.where(deg > 0, jax.lax.rsqrt(jnp.maximum(deg, 1.0)), 0.0)
            return (src, dst, deg_inv_sqrt)
        key = jax.random.key(seed)
        ks = jax.random.split(key, 8)
        node_fts = jax.random.normal(ks[0], (N_NODES, D), dtype=jnp.float32)
        edge_index = jax.random.randint(ks[1], (2, 25000), 0, N_NODES, dtype=jnp.int64)
        scale = 1.0 / np.sqrt(D)
        W1 = jax.random.uniform(ks[2], (D, D), jnp.float32, -scale, scale)
        b1 = jnp.zeros((D,), jnp.float32)
        W2 = jax.random.uniform(ks[3], (D, D), jnp.float32, -scale, scale)
        b2 = jnp.zeros((D,), jnp.float32)
        W3 = jax.random.uniform(ks[4], (D, D), jnp.float32, -scale, scale)
        b3 = jnp.zeros((D,), jnp.float32)
        return {'node_fts': node_fts, 'edge_index': edge_index, 'W1': W1, 'b1': b1, 'W2': W2, 'b2': b2, 'W3': W3, 'b3': b3}
    _L0_gnn_all = _L0_gnn_setup()
    _L0_gnn_in = {k: v for k, v in _L0_gnn_all.items() if k in ('W1', 'b1', 'W2', 'b2', 'W3', 'b3')}
    del _L0_gnn_all

    def _L1_gnn_setup():
        import jax, jax.numpy as jnp
        import numpy as np
        N_NODES = 50000
        N_EDGES = 12500
        D = 128
        EPS = 1e-12
        key = jax.random.key(seed)
        ks = jax.random.split(key, 12)
        s = 1.0 / np.sqrt(D)
        return {'node_features': jax.random.normal(ks[0], (N_NODES, D), jnp.float32), 'edge_features': jax.random.normal(ks[1], (N_EDGES, D), jnp.float32), 'src': jax.random.randint(ks[2], (N_EDGES,), 0, N_NODES, jnp.int32), 'dst': jax.random.randint(ks[3], (N_EDGES,), 0, N_NODES, jnp.int32), 'edge_weight_raw': jax.random.uniform(ks[4], (N_EDGES,), jnp.float32), 'W_pool': jax.random.normal(ks[5], (D, D), jnp.float32) * s, 'b_pool': jnp.zeros((D,), jnp.float32), 'W1_self': jax.random.normal(ks[6], (D, D), jnp.float32) * s, 'W1_neigh': jax.random.normal(ks[7], (D, D), jnp.float32) * s, 'b1': jnp.zeros((D,), jnp.float32), 'W2_self': jax.random.normal(ks[8], (D, D), jnp.float32) * s, 'W2_neigh': jax.random.normal(ks[9], (D, D), jnp.float32) * s, 'b2': jnp.zeros((D,), jnp.float32)}
    _L1_gnn_all = _L1_gnn_setup()
    _L1_gnn_in = {k: v for k, v in _L1_gnn_all.items() if k in ('W_pool', 'b_pool', 'W1_self', 'W1_neigh', 'b1', 'W2_self', 'W2_neigh', 'b2')}
    del _L1_gnn_all
    return {'x': x, 'src': src, 'dst': dst, 'edge_attr_128': edge_attr_128, 'edge_weight': edge_weight, 'L0_gnn_W1': _L0_gnn_in['W1'], 'L0_gnn_b1': _L0_gnn_in['b1'], 'L0_gnn_W2': _L0_gnn_in['W2'], 'L0_gnn_b2': _L0_gnn_in['b2'], 'L0_gnn_W3': _L0_gnn_in['W3'], 'L0_gnn_b3': _L0_gnn_in['b3'], 'L1_gnn_W_pool': _L1_gnn_in['W_pool'], 'L1_gnn_b_pool': _L1_gnn_in['b_pool'], 'L1_gnn_W1_self': _L1_gnn_in['W1_self'], 'L1_gnn_W1_neigh': _L1_gnn_in['W1_neigh'], 'L1_gnn_b1': _L1_gnn_in['b1'], 'L1_gnn_W2_self': _L1_gnn_in['W2_self'], 'L1_gnn_W2_neigh': _L1_gnn_in['W2_neigh'], 'L1_gnn_b2': _L1_gnn_in['b2']}

def reference(x, src, dst, edge_attr_128, edge_weight, L0_gnn_W1, L0_gnn_b1, L0_gnn_W2, L0_gnn_b2, L0_gnn_W3, L0_gnn_b3, L1_gnn_W_pool, L1_gnn_b_pool, L1_gnn_W1_self, L1_gnn_W1_neigh, L1_gnn_b1, L1_gnn_W2_self, L1_gnn_W2_neigh, L1_gnn_b2):
    import jax
    import jax.numpy as jnp

    def _L0_gnn_ref(node_fts, edge_index, W1, b1, W2, b2, W3, b3):
        import jax, jax.numpy as jnp
        import numpy as np
        N_NODES = 100000
        D = 128

        def gcn_conv(x, W, b, src, dst, deg_inv_sqrt):
            h = x @ W
            norm = deg_inv_sqrt[src] * deg_inv_sqrt[dst]
            msgs = h[src] * norm[:, None]
            out = jax.ops.segment_sum(msgs, dst, num_segments=x.shape[0])
            return out + b

        def _prep_edges(edge_index, n_nodes):
            loops = jnp.arange(n_nodes, dtype=edge_index.dtype)
            src = jnp.concatenate([edge_index[0], loops])
            dst = jnp.concatenate([edge_index[1], loops])
            deg = jax.ops.segment_sum(jnp.ones_like(dst, dtype=jnp.float32), dst, num_segments=n_nodes)
            deg_inv_sqrt = jnp.where(deg > 0, jax.lax.rsqrt(jnp.maximum(deg, 1.0)), 0.0)
            return (src, dst, deg_inv_sqrt)
        n = node_fts.shape[0]
        src, dst, dinv = _prep_edges(edge_index, n)
        x = jax.nn.relu(gcn_conv(node_fts, W1, b1, src, dst, dinv))
        x = jax.nn.relu(gcn_conv(x, W2, b2, src, dst, dinv))
        x = jax.nn.relu(gcn_conv(x, W3, b3, src, dst, dinv))
        return x

    def _L1_gnn_ref(node_features, edge_features, src, dst, edge_weight_raw, W_pool, b_pool, W1_self, W1_neigh, b1, W2_self, W2_neigh, b2):
        import jax, jax.numpy as jnp
        import numpy as np
        N_NODES = 50000
        N_EDGES = 12500
        D = 128
        EPS = 1e-12
        N = node_features.shape[0]
        deg = jax.ops.segment_sum(jnp.ones_like(edge_weight_raw), dst, num_segments=N)
        wsum = jax.ops.segment_sum(edge_weight_raw, dst, num_segments=N)
        w = edge_weight_raw / jnp.maximum(wsum, EPS)[dst]
        feat = jax.nn.relu(node_features @ W_pool + b_pool)
        msg = feat[src] * w[:, None]
        neigh = jax.ops.segment_max(msg, dst, num_segments=N)
        neigh = jnp.where(deg[:, None] > 0, neigh, 0.0)
        rst = node_features @ W1_self + neigh @ W1_neigh + b1
        nrm = jnp.linalg.norm(rst, axis=1, keepdims=True)
        rst = rst / jnp.maximum(nrm, EPS)
        h = jax.nn.relu(rst)
        msg2 = h[src] * w[:, None]
        neigh2 = jax.ops.segment_sum(msg2, dst, num_segments=N) / jnp.maximum(deg, 1.0)[:, None]
        out = jax.nn.relu(h @ W2_self + neigh2 @ W2_neigh + b2)
        return out
    edge_index = jnp.stack([src, dst])
    h = jnp.maximum(_layernorm(x, axis=-1), 0.0)
    x = x + _L0_gnn_ref(h, edge_index, L0_gnn_W1, L0_gnn_b1, L0_gnn_W2, L0_gnn_b2, L0_gnn_W3, L0_gnn_b3)
    h = jnp.maximum(_layernorm(x, axis=-1), 0.0)
    x = x + _L1_gnn_ref(h, edge_attr_128, src, dst, edge_weight, L1_gnn_W_pool, L1_gnn_b_pool, L1_gnn_W1_self, L1_gnn_W1_neigh, L1_gnn_b1, L1_gnn_W2_self, L1_gnn_W2_neigh, L1_gnn_b2)
    return x

_drawn_inputs = setup_inputs


def setup_inputs(seed=0):
    import zlib

    import numpy as np

    out = dict(_drawn_inputs(seed))
    spreads = {'L0_gnn_b1': (0.0, 0.704),
     'L0_gnn_b2': (0.0, 0.1),
     'L0_gnn_b3': (0.0, 0.1),
     'L1_gnn_b_pool': (0.0, 0.8),
     'L1_gnn_b1': (0.0, 0.8),
     'L1_gnn_b2': (0.0, 0.1)}
    factors = {'edge_weight': 8.0,
     'L1_gnn_W_pool': 6.541,
     'L1_gnn_W1_neigh': 6.318,
     'L1_gnn_W2_neigh': 3.395}
    for name, (base, spread) in spreads.items():
        noise = np.random.default_rng([zlib.crc32(name.encode()), seed]).standard_normal(out[name].shape)
        drawn = base * np.exp(spread * noise) if base else spread * noise
        out[name] = jnp.asarray(drawn.astype(out[name].dtype))
    for name, factor in factors.items():
        out[name] = (out[name] * factor).astype(out[name].dtype)
    return out
```

```python
import numpy as np
import concourse.bass as bass
from concourse import mybir
from contextlib import ExitStack

F32 = mybir.dt.float32
BF16 = mybir.dt.bfloat16
I32 = mybir.dt.int32
U32 = mybir.dt.uint32
ALU = mybir.AluOpType
ACT = mybir.ActivationFunctionType

P = 128
TILES = 4
ROWS = P * TILES
RING = 4
LN_EPS = 1e-5
NORM_EPS = 1e-12
FAR = 3.0e38


class Turn:

    def __init__(self, g, r, s):
        self.g, self.r, self.s = g, r, s


class Step:

    def __init__(self, i, u, n):
        self.i, self.u, self.n = i, u, n

    def _plus(self, c):
        v = RING * self.i + c
        return min(max(v, 0), self.n) if isinstance(self.i, int) else v

    def at(self, lag):
        c = self.u - lag
        if isinstance(self.i, int):
            g = RING * self.i + c
            return Turn(g, g // RING, g % RING) if 0 <= g < self.n else None
        return Turn(RING * self.i + c, self.i + c // RING, c % RING)

    def through(self, lag):
        return self._plus(self.u - lag + 1)

    def before(self, lag):
        return self._plus(self.u - lag)


def pipeline(engine, n, last_lag, step):
    head = -(-last_lag // RING)
    tail = (n - 1) // RING
    for t in range(head * RING):
        step(Step(t // RING, t % RING, n))
    with engine.Fori(head, tail) as i:
        for u in range(RING):
            step(Step(i, u, n))
    for t in range(tail * RING, n + last_lag):
        step(Step(t // RING, t % RING, n))


def gnn_kernel(nc, x, src, dst, edge_weight, W, B, out):
    N, D = x.shape
    E = src.shape[0]
    assert D == P
    NODE_GROUPS = -(-N // ROWS)

    ctx = ExitStack()
    with ctx:
        def sb(name, shape, dt=F32):
            return ctx.enter_context(nc.sbuf_tensor(name, shape, dt))

        def sem(name):
            return ctx.enter_context(nc.semaphore(name))

        def flat(t):
            return t.rearrange("p j d -> p (j d)")

        def per_row(col):
            return col.unsqueeze(2).broadcast_to([P, TILES, P])

        stages, ring_places, started = {}, {}, {}

        def stage(name):
            if name not in stages:
                stages[name] = sem(f"done_{name}")
            return stages[name]

        def ring_sems(name):
            if name not in ring_places:
                ring_places[name] = [sem(f"{name}_{s}") for s in range(RING)]
            return ring_places[name]

        def wait(engine, semaphore, value):
            if isinstance(value, int) and value <= 0:
                return
            engine.wait_ge(semaphore, value + started.get(semaphore.name, 0))

        def uses(n, s):
            return len(range(s, n, RING))

        def passed(n, names, rings):
            for name in names:
                k = stages[name].name
                started[k] = started.get(k, 0) + n
            for name, each in rings.items():
                for s in range(RING):
                    k = ring_places[name][s].name
                    started[k] = started.get(k, 0) + each * uses(n, s)

        ring = [sb(f"ring{i}", [P, RING, TILES, P]) for i in range(8)]
        buf = [sb(f"buf{i}", [P, TILES, P]) for i in range(10)]
        junk = sb("junk", [P, TILES, P])
        bank = [ctx.enter_context(nc.psum_tensor(f"bank{i}", [P, ROWS], F32)) for i in range(8)]

        w_sb = {k: sb(f"w_{k}", [P, P]) for k in W}
        w_in = sem("w_in")
        ident = sb("ident", [P, P])
        zeros_done, ident_done, ones3_done = sem("zeros_done"), sem("ident_done"), sem("ones3_done")
        ones3 = sb("ones3", [3, P], BF16)
        bias_col = sb("bias_col", [P, 2])
        bias_in = sem("bias_in")
        ROW_BIASES = ("gcn3", "pool", "one", "two")
        bias_row = sb("bias_row", [1, len(ROW_BIASES), P])
        bias_rest = sb("bias_rest", [1, 2, len(ROW_BIASES), P])
        bias_part = [sb(f"bias_part{k}", [1, len(ROW_BIASES), P], BF16) for k in range(3)]
        bias3 = sb("bias3", [3, len(ROW_BIASES), TILES, P], BF16)
        bias_split, bias3_in = sem("bias_split"), sem("bias3_in")
        eps_col = sb("eps_col", [P, 1])
        eps_done = sem("eps_done")

        def const_dve(dve):
            dve.memset(eps_col[:, :], LN_EPS).then_inc(eps_done, 1)
            dve.wait_ge(bias_in, 16 * (2 + len(ROW_BIASES)))
            n = 0
            rest = bias_row[:, :, :]
            for k in range(3):
                dve.tensor_copy(bias_part[k][:, :, :], rest).then_inc(bias_split, 1)
                n += 1
                if k < 2:
                    dve.wait_ge(bias_split, n)
                    dve.tensor_tensor(bias_rest[:, k, :, :], rest, bias_part[k][:, :, :],
                                      ALU.subtract).then_inc(bias_split, 1)
                    n += 1
                    dve.wait_ge(bias_split, n)
                    rest = bias_rest[:, k, :, :]

        BIAS_SPLIT_ALL = 5

        NG = NODE_GROUPS
        x_ring, xx_ring, o_ring = ring[0:3]
        n_stats = sb("n_stats", [P, 2, TILES, 6])
        n_mv = sb("n_mv", [P, 2, 2, TILES, 2])
        n_sd = sb("n_sd", [P, 3, TILES])
        n_rs = sb("n_rs", [P, 3, 2, TILES])
        n_c, n_y, n_h = buf[0:2], buf[2:4], buf[4]
        n_ss = sb("n_ss", [P, TILES])
        n_nm = sb("n_nm", [P, TILES])
        n_t = dict(zip("z12gh", (flat(b[:, :, :]) for b in buf[5:10])))

        n_loaded, n_stored = ring_sems("loaded"), ring_sems("stored")
        names = ("bn ag sd s1 ce1 no1 bn2 ag2 sd2 rs2 c2 y2 TB zBT m1 x1T m2 x2T m3 xx Tg gT mr sq sd3 nm rs3 h "
                 "T3 hT m5 fin").split()
        S = {k: stage(k) for k in names}

        def rows_of(turn, ap):
            if isinstance(turn.g, int) and turn.g == NG - 1:
                a = ap[N - ROWS:N, :]
            else:
                a = ap[bass.ds(turn.g * ROWS, ROWS), :]
            return a.rearrange("(p j) d -> p (j d)", p=P)

        def node_sp(sp):
            def step(t):
                if c := t.at(0):
                    wait(sp, S["xx"], t.through(0) - RING)
                    sp.dma_start(flat(x_ring[:, c.s, :, :]), rows_of(c, x)).then_inc(n_loaded[c.s], 16)
                if c := t.at(8):
                    wait(sp, S["fin"], t.through(8))
                    if isinstance(c.g, int) and c.g == NG - 1:
                        p = (NG - 2) % RING
                        wait(sp, n_stored[p], 16 * ((NG - 2) // RING + 1))
                    sp.dma_start(rows_of(c, out), flat(o_ring[:, c.s, :, :])).then_inc(n_stored[c.s], 16)
            pipeline(sp, NG, 8, step)
            for s in range(RING):
                wait(sp, n_stored[s], 16 * uses(NG, s))

        def node_dve(dve):
            def stats(c, src_ring, k, bn):
                for j in range(TILES):
                    last = dve.bn_stats(n_stats[:, k, j, :], src_ring[:, c.s, j, :])
                last.then_inc(S[bn], 1)

            def moments(c, k, ag):
                for j in range(TILES):
                    last = dve.bn_aggr(n_mv[:, k, c.s % 2, j, :], n_stats[:, k, j, :])
                last.then_inc(S[ag], 1)

            def step(t):
                if c := t.at(1):
                    wait(dve, n_loaded[c.s], 16 * (c.r + 1))
                    wait(dve, S["ag"], t.before(1))
                    stats(c, x_ring, 0, "bn")
                wait(dve, S["bn"], t.through(1))
                wait(dve, S["sd"], t.before(1) - 1)
                wait(dve, S["ce1"], t.before(1) - 1)
                if c := t.at(7):
                    wait(dve, S["sd3"], t.through(7))
                    dve.tensor_scalar(n_nm[:, :], n_sd[:, 2, :], NORM_EPS, None, ALU.max).then_inc(S["nm"], 1)
                if c := t.at(1):
                    moments(c, 0, "ag")
                if c := t.at(7):
                    wait(dve, S["nm"], t.through(7))
                    dve.reciprocal(n_rs[:, 2, 0, :], n_nm[:, :]).then_inc(S["rs3"], 1)
                    wait(dve, S["rs3"], t.through(7))
                    wait(dve, S["T3"], t.before(7))
                    dve.tensor_tensor(n_h[:, :, :], bank[6][:, :].rearrange("p (j d) -> p j d", j=TILES),
                                      per_row(n_rs[:, 2, 0, :]), ALU.mult).then_inc(S["h"], 1)
                if c := t.at(4):
                    wait(dve, S["m3"], t.through(4))
                    wait(dve, S["fin"], t.through(4) - RING)
                    dve.scalar_tensor_tensor(out=flat(xx_ring[:, c.s, :, :]), in0=bank[3][:, :], scalar=0.0,
                                             in1=flat(x_ring[:, c.s, :, :]), op0=ALU.max,
                                             op1=ALU.add).then_inc(S["xx"], 1)
                    wait(dve, S["xx"], t.through(4))
                    wait(dve, S["ag2"], t.before(4))
                    stats(c, xx_ring, 1, "bn2")
                wait(dve, S["bn2"], t.through(4))
                wait(dve, S["sd2"], t.before(4) - 1)
                wait(dve, S["c2"], t.before(4) - 1)
                if c := t.at(1):
                    wait(dve, S["sd"], t.through(1))
                    wait(dve, S["no1"], t.before(1) - 1)
                    dve.reciprocal(n_rs[:, 0, c.s % 2, :], n_sd[:, 0, :]).then_inc(S["s1"], 1)
                if c := t.at(4):
                    moments(c, 1, "ag2")
                if c := t.at(7):
                    wait(dve, S["m5"], t.through(7))
                    wait(dve, n_stored[c.s], 16 * c.r)
                    dve.scalar_tensor_tensor(out=flat(o_ring[:, c.s, :, :]), in0=bank[7][:, :], scalar=0.0,
                                             in1=flat(xx_ring[:, c.s, :, :]), op0=ALU.max,
                                             op1=ALU.add).then_inc(S["fin"], 1)
                if c := t.at(4):
                    wait(dve, S["sd2"], t.through(4))
                    wait(dve, S["y2"], t.before(4) - 1)
                    dve.reciprocal(n_rs[:, 1, c.s % 2, :], n_sd[:, 1, :]).then_inc(S["rs2"], 1)
            pipeline(dve, NG, 8, step)

        def node_pool(pool):
            def norm(c, src_ring, k, ag, rs, ce, no, T, value, before):
                wait(pool, S[ag], value)
                wait(pool, S[no], before)
                pool.tensor_tensor(n_c[k][:, :, :], src_ring[:, c.s, :, :], per_row(n_mv[:, k, c.s % 2, :, 0]),
                                   ALU.subtract).then_inc(S[ce], 1)
                wait(pool, S[rs], value)
                wait(pool, S[ce], value)
                wait(pool, S[T], before)
                pool.tensor_tensor(n_y[k][:, :, :], n_c[k][:, :, :], per_row(n_rs[:, k, c.s % 2, :]),
                                   ALU.mult).then_inc(S[no], 1)

            def step(t):
                if c := t.at(5):
                    norm(c, xx_ring, 1, "ag2", "rs2", "c2", "y2", "Tg", t.through(5), t.before(5))
                if c := t.at(2):
                    norm(c, x_ring, 0, "ag", "s1", "ce1", "no1", "TB", t.through(2), t.before(2))
            pipeline(pool, NG, 8, step)

        def node_act(act):
            def step(t):
                if c := t.at(4):
                    wait(act, S["m2"], t.through(4))
                    wait(act, S["m3"], t.before(4))
                    act.activation(n_t["2"], bank[2][:, :], ACT.Relu,
                                   bias=bias_col[:, 1:2]).then_inc(S["x2T"], 1)
                if c := t.at(3):
                    wait(act, S["TB"], t.through(3))
                    wait(act, S["m1"], t.before(3))
                    act.activation(n_t["z"], bank[0][:, :], ACT.Relu).then_inc(S["zBT"], 1)
                if c := t.at(6):
                    wait(act, S["Tg"], t.through(6))
                    wait(act, S["mr"], t.before(6))
                    act.activation(n_t["g"], bank[4][:, :], ACT.Relu).then_inc(S["gT"], 1)
                if c := t.at(7):
                    wait(act, S["T3"], t.through(7))
                    wait(act, S["m5"], t.before(7))
                    act.activation(n_t["h"], bank[5][:, :], ACT.Relu).then_inc(S["hT"], 1)
                if c := t.at(3):
                    wait(act, S["m1"], t.through(3))
                    wait(act, S["m2"], t.before(3))
                    act.activation(n_t["1"], bank[1][:, :], ACT.Relu,
                                   bias=bias_col[:, 0:1]).then_inc(S["x1T"], 1)
                if c := t.at(1):
                    wait(act, S["ag"], t.through(1))
                    wait(act, S["s1"], t.before(1))
                    act.activation(n_sd[:, 0, :], n_mv[:, 0, c.s % 2, :, 1], ACT.Sqrt,
                                   bias=eps_col[:, 0:1]).then_inc(S["sd"], 1)
                if c := t.at(6):
                    wait(act, S["mr"], t.through(6))
                    wait(act, S["sd3"], t.before(6))
                    for j in range(TILES):
                        last = act.activation(junk[:, j, :], bank[6][:, j * P:(j + 1) * P], ACT.Square,
                                              accum_out=n_ss[:, j:j + 1])
                    last.then_inc(S["sq"], 1)
                    wait(act, S["sq"], t.through(6))
                    wait(act, S["nm"], t.before(6))
                    act.activation(n_sd[:, 2, :], n_ss[:, :], ACT.Sqrt).then_inc(S["sd3"], 1)
                if c := t.at(4):
                    wait(act, S["ag2"], t.through(4))
                    wait(act, S["rs2"], t.before(4))
                    act.activation(n_sd[:, 1, :], n_mv[:, 1, c.s % 2, :, 1], ACT.Sqrt,
                                   bias=eps_col[:, 0:1]).then_inc(S["sd2"], 1)
            act.wait_ge(eps_done, 1)
            act.wait_ge(bias_in, 16 * (2 + len(ROW_BIASES)))
            pipeline(act, NG, 8, step)

        def node_pe(pe):
            def step(t):
                if c := t.at(3):
                    wait(pe, S["no1"], t.through(3))
                    wait(pe, S["zBT"], t.before(3))
                    transposes(pe, 0, n_y[0], S["TB"])
                if c := t.at(6):
                    wait(pe, S["y2"], t.through(6))
                    wait(pe, S["gT"], t.before(6))
                    transposes(pe, 4, n_y[1], S["Tg"])
                if c := t.at(4):
                    wait(pe, S["x2T"], t.through(4))
                    wait(pe, S["xx"], t.before(4))
                    rows_matmul(pe, 3, n_t["2"], "gcn3", "gcn3", S["m3"])
                if c := t.at(3):
                    wait(pe, S["zBT"], t.through(3))
                    wait(pe, S["x1T"], t.before(3))
                    pe.matmul(bank[1][:, :], w_sb["gcn1"][:, :], n_t["z"], start=True, stop=True).then_inc(S["m1"], 1)
                if c := t.at(7):
                    wait(pe, S["h"], t.through(7))
                    wait(pe, S["hT"], t.before(7))
                    transposes(pe, 5, n_h, S["T3"])
                if c := t.at(6):
                    wait(pe, S["gT"], t.through(6))
                    wait(pe, S["h"], t.before(6))
                    rows_matmul(pe, 6, n_t["g"], "self1", "one", S["mr"])
                if c := t.at(7):
                    wait(pe, S["hT"], t.through(7))
                    wait(pe, S["fin"], t.before(7))
                    rows_matmul(pe, 7, n_t["h"], "self2", "two", S["m5"])
                if c := t.at(3):
                    wait(pe, S["x1T"], t.through(3))
                    wait(pe, S["x2T"], t.before(3))
                    pe.matmul(bank[2][:, :], w_sb["gcn2"][:, :], n_t["1"], start=True, stop=True).then_inc(S["m2"], 1)
            pipeline(pe, NG, 8, step)

        EG = -(-E // ROWS)
        EP = EG * ROWS
        ET = EP // P
        CW = 2 * P
        CR = EP // CW
        CF, CT = E // CW, E % CW
        assert EP % CW == 0 and CT > 0 and CF == CR - 1

        def scratch(name, shape, dt=F32):
            return nc.dram_tensor(name, shape, dt, kind="Internal").ap()

        node_table = scratch("node_table", [N, 2])
        table = {k: scratch(f"table{k}", [2 * EP, P]) for k in (1, 2, 3, 4)}
        self_rows = [scratch(f"self_rows{k}", [EP, P]) for k in range(2)]
        x_dst = scratch("x_dst", [EP, P])
        xx_dst = scratch("xx_dst", [EP, P])
        segment_rows = scratch("segment_rows", [2, EP], BF16)
        carry_a = scratch("carry_a", [CR, 3])
        carry_b = scratch("carry_b", [2, CR])

        DINV, WEIGHT, CINV, CD, OWN = range(5)
        edge_f = sb("edge_f", [P, ET, 5])
        SRC, DST, SCAT, TAB = range(4)
        edge_i = sb("edge_i", [P, ET, 4], I32)
        bias_bc = {k: sb(f"bias_bc_{k}", [P, P]) for k in ("gcn1", "gcn2", "gcn3")}
        bias_bc_in = sem("bias_bc_in")

        q_int = sb("q_int", [CR, 2, CW], I32)
        q_ends = sb("q_ends", [CR, 2], I32)
        q_d = sb("q_d", [CR, CW + 2])
        Q = {k: sb(f"q_{k}", [CR, CW]) for k in
             ("same last ones cnt ws pm cntF wsF deg sd y y2 y3 wmax").split()}
        q_out = sb("q_out", [CR, 7, CW])
        q_seg = sb("q_seg", [CR, 2, CW], BF16)
        q_carry = sb("q_carry", [CR, 3])
        q_row = sb("q_row", [1, 3, CR])
        q_full = sb("q_full", [1, 2, CR])
        q_in = sb("q_in", [CR, 2])
        own_i = sb("own_i", [P, ET], I32)
        q_zero = buf[0]
        p_set, p_load, p_dve, p_act, p_seg, p_c1, p_c2, p_c3, p_c4, p_T, p_own, p_q, p_deg, p_table0 = (
            sem(f"p_{k}") for k in "set load dve act seg c1 c2 c3 c4 T own q deg table0".split())
        N_SET = 9
        FILL = N // P * 2

        def prep_pool(pool):
            pool.memset(q_int[:, 0, :], 0).then_inc(p_set, 1)
            pool.memset(q_int[:, 1, :], N).then_inc(p_set, 1)
            pool.memset(q_ends[:, 0:1], -1).then_inc(p_set, 1)
            pool.memset(q_ends[:, 1:2], N + 1).then_inc(p_set, 1)
            pool.memset(q_out[:, 3, :], 0.0).then_inc(p_set, 1)
            pool.memset(Q["ones"][:, :], 1.0).then_inc(p_set, 1)
            pool.memset(q_in[:, :], 0.0).then_inc(p_set, 1)
            pool.memset(flat(q_zero[:, :, :]), 0.0).then_inc(p_set, 1)
            pool.memset(edge_i[:, :, TAB], 0).then_inc(p_set, 1)
            pool.iota(own_i[:, :], pattern=[[P, ET]], base=EP, channel_multiplier=1).then_inc(p_own, 1)

        def prep_sp(sp):
            sp.wait_ge(p_set, N_SET)
            grid = [a[0:CF * CW].rearrange("(r c) -> r c", c=CW) for a in (src, dst, edge_weight)]
            rest = [a[CF * CW:E].rearrange("(a c) -> a c", a=1) for a in (src, dst, edge_weight)]
            for k in range(3):
                to = q_int[:, k, :] if k < 2 else q_out[:, 3, :]
                sp.dma_start(to[0:CF, :], grid[k]).then_inc(p_load, 16)
                sp.dma_start(to[CF:CR, 0:CT], rest[k]).then_inc(p_load, 16)
            sp.dma_start(q_ends[1:CR, 0:1], grid[1][:, CW - 1:CW], allow_slow_non_contiguous=True).then_inc(p_load, 16)
            sp.dma_start(q_ends[0:CF - 1, 1:2], grid[1][1:CF, 0:1], allow_slow_non_contiguous=True).then_inc(p_load, 16)
            sp.dma_start(q_ends[CF - 1:CF, 1:2], rest[1][:, 0:1], allow_slow_non_contiguous=True).then_inc(p_load, 16)
            flat_table = node_table.rearrange("n k -> (n k)")
            part = flat_table[0:P * FILL].rearrange("(p c) -> p c", c=FILL)
            zero = flat(q_zero[:, :, :])
            n = 0
            for c in range(0, FILL, ROWS):
                w = min(ROWS, FILL - c)
                sp.dma_start(part[:, c:c + w], zero[:, 0:w]).then_inc(p_table0, 16)
                n += 1
            tail = N * 2 - P * FILL
            if tail:
                sp.dma_start(flat_table[P * FILL:N * 2].rearrange("(a c) -> a c", a=1), zero[0:1, 0:tail])\
                  .then_inc(p_table0, 16)
                n += 1
            sp.wait_ge(p_seg, 1)
            for k in range(2):
                sp.dma_start(segment_rows[k, :].rearrange("(r c) -> r c", c=CW), q_seg[:, k, :]).then_inc(p_c4, 16)
            sp.wait_ge(p_c1, 1)
            sp.dma_start(carry_a, q_carry[:, :]).then_inc(p_c2, 16)
            sp.wait_ge(p_c2, 16)
            sp.dma_start(q_row[:, :, :], carry_a.rearrange("(a r) k -> a k r", a=1), allow_slow_non_contiguous=True).then_inc(p_c2, 16)
            sp.wait_ge(p_c1, 2)
            sp.dma_start(carry_b.rearrange("(a k) r -> a k r", a=1), q_full[:, :, :]).then_inc(p_c3, 16)
            sp.wait_ge(p_c3, 16)
            sp.dma_start(q_in[1:CR, :], carry_b[:, 0:CR - 1].rearrange("k r -> r k"), allow_slow_non_contiguous=True).then_inc(p_c3, 16)
            sp.wait_ge(p_c3, 32)
            sp.wait_ge(p_c4, 32)
            sp.wait_ge(p_table0, 16 * n)

        def prep_dve(dve):
            count = [0]

            def chain(ins):
                count[0] += 1
                ins.then_inc(p_dve, 1)
                dve.wait_ge(p_dve, count[0])

            dve.wait_ge(p_load, 16 * 9)
            dve.wait_ge(p_set, N_SET)
            dve.tensor_copy(q_d[:, 0:1], q_ends[:, 0:1])
            dve.tensor_copy(q_d[:, CW + 1:CW + 2], q_ends[:, 1:2])
            chain(dve.tensor_copy(q_d[:, 1:CW + 1], q_int[:, 1, :]))
            d = q_d[:, 1:CW + 1]
            dve.tensor_tensor(Q["last"][:, :], d, q_d[:, 2:CW + 2], ALU.not_equal)
            chain(dve.tensor_tensor(Q["same"][:, :], d, q_d[:, 0:CW], ALU.is_equal))
            dve.tensor_copy(q_seg[:, 0, :], Q["same"][:, :])
            dve.tensor_scalar(q_seg[:, 1, :], Q["same"][:, :], -1.0, FAR, ALU.add, ALU.mult).then_inc(p_seg, 1)
            w = q_out[:, 3, :]
            dve.tensor_tensor_scan(Q["cnt"][:, :], Q["same"][:, :], Q["ones"][:, :], 0.0, ALU.mult, ALU.add)
            dve.tensor_tensor_scan(Q["ws"][:, :], Q["same"][:, :], w, 0.0, ALU.mult, ALU.add)
            chain(dve.tensor_tensor_scan(Q["pm"][:, :], Q["same"][:, :], Q["ones"][:, :], 1.0, ALU.mult, ALU.mult))
            for k, name in enumerate(("cnt", "ws", "pm")):
                last = dve.tensor_copy(q_carry[:, k:k + 1], Q[name][:, CW - 1:CW])
            last.then_inc(p_c1, 1)
            dve.tensor_copy(q_out[:, 0, :], q_int[:, 0, :])
            dve.tensor_scalar(q_out[:, 1, :], d, float(N - 1), None, ALU.min)
            chain(dve.scalar_tensor_tensor(out=Q["y3"][:, :], in0=Q["last"][:, :], scalar=-2.0 * N, in1=d,
                                           op0=ALU.mult, op1=ALU.add))
            chain(dve.tensor_scalar(q_out[:, 2, :], Q["y3"][:, :], 2.0 * N, None, ALU.add))
            dve.wait_ge(p_c2, 32)
            for k in range(2):
                last = dve.tensor_tensor_scan(q_full[:, k, :], q_row[:, 2, :], q_row[:, k, :], 0.0, ALU.mult, ALU.add)
            last.then_inc(p_c1, 1)
            dve.wait_ge(p_c3, 32)
            for k, (a, b) in enumerate((("cnt", "cntF"), ("ws", "wsF"))):
                op = dve.scalar_tensor_tensor(out=Q[b][:, :], in0=Q["pm"][:, :], scalar=q_in[:, k:k + 1],
                                              in1=Q[a][:, :], op0=ALU.mult, op1=ALU.add)
            chain(op)
            dve.tensor_scalar(Q["wmax"][:, :], Q["wsF"][:, :], NORM_EPS, None, ALU.max)
            dve.tensor_scalar(Q["deg"][:, :], Q["cntF"][:, :], 1.0, None, ALU.add).then_inc(p_deg, 1)
            dve.wait_ge(p_act, 1)
            dve.reciprocal(q_out[:, 5, :], Q["wmax"][:, :])
            dve.reciprocal(Q["y3"][:, :], Q["cntF"][:, :])
            chain(dve.reciprocal(Q["y"][:, :], Q["sd"][:, :]))
            dve.tensor_tensor(q_out[:, 6, :], q_out[:, 5, :], Q["y3"][:, :], ALU.mult)
            chain(dve.tensor_tensor(Q["y2"][:, :], Q["y"][:, :], Q["y"][:, :], ALU.mult))
            chain(dve.tensor_tensor(Q["y3"][:, :], Q["y2"][:, :], Q["deg"][:, :], ALU.mult))
            chain(dve.tensor_scalar(Q["y2"][:, :], Q["y3"][:, :], -0.5, 1.5, ALU.mult, ALU.add))
            dve.tensor_tensor(q_out[:, 4, :], Q["y"][:, :], Q["y2"][:, :], ALU.mult).then_inc(p_q, 1)
            dve.wait_ge(p_T, 14)
            dve.wait_ge(p_own, 1)
            for a in range(7):
                for k in range(2):
                    n = 2 * a + k
                    col = bank[n // 5][:, (n % 5) * CR:(n % 5) * CR + CR]
                    to = edge_i[:, k::2, a] if a < 3 else edge_f[:, k::2, {3: WEIGHT, 4: DINV, 5: CINV, 6: CD}[a]]
                    dve.tensor_copy(to, col)
            dve.tensor_copy(edge_f[:, :, OWN], own_i[:, :])

        def prep_act(act):
            act.wait_ge(p_deg, 1)
            act.activation(Q["sd"][:, :], Q["deg"][:, :], ACT.Sqrt).then_inc(p_act, 1)

        def prep_pe(pe):
            pe.wait_ge(p_q, 1)
            for a in range(7):
                for k in range(2):
                    n = 2 * a + k
                    pe.transpose(bank[n // 5][:, (n % 5) * CR:(n % 5) * CR + CR],
                                 q_out[:, a, k * P:(k + 1) * P], ident[0:CR, 0:CR]).then_inc(p_T, 1)

        st_i = sb("st_i", [P, RING, TILES, 4], I32)
        st_f = sb("st_f", [P, RING, TILES, 5])
        t_val = sb("t_val", [P, RING, TILES, 2])
        t_staged = stage("staged")
        t_scattered = ring_sems("scattered")

        def group_of(per_edge, c):
            return per_edge[:, bass.ds(c.g * TILES, TILES), :]

        def table_dve(dve):
            def step(t):
                if c := t.at(0):
                    wait(dve, t_scattered[c.s], 16 * TILES * c.r)
                    dve.tensor_copy(st_i[:, c.s, :, :], group_of(edge_i, c))
                    dve.tensor_scalar(t_val[:, c.s, :, 0], edge_f[:, bass.ds(c.g * TILES, TILES), OWN],
                                      -float(EP), None, ALU.add)
                    dve.tensor_copy(t_val[:, c.s, :, 1], edge_f[:, bass.ds(c.g * TILES, TILES), DINV])\
                       .then_inc(t_staged, 1)
            pipeline(dve, EG, 1, step)

        def table_pool(pool):
            limit = Limit(pool, node_table)

            def step(t):
                if c := t.at(1):
                    wait(pool, t_staged, t.through(1))
                    limit.set()
                    for j in range(TILES):
                        pool.indirect_dma_start(
                            out=node_table, out_offset=bass.IndirectOffsetOnAxis(ap=st_i[:, c.s, j, SCAT:SCAT + 1], axis=0),
                            in_=t_val[:, c.s, j, :], in_offset=None, bounds_check=limit.register,
                            oob_is_err=False).then_inc(t_scattered[c.s], 16)
            pipeline(pool, EG, 1, step)
            for s in range(RING):
                wait(pool, t_scattered[s], 16 * TILES * uses(EG, s))

        xs_ring, xd_ring, t1b_ring, t2b_ring, t3b_ring, t4b_ring, z1_ring, r_ring = ring
        (f_zA, f_zB, f_zAT, f_zBT, f_S, f_U, f_v, f_x1T, f_x2T, f_y2) = buf
        more = [sb(f"more{i}", [P, TILES, P]) for i in range(5)]
        (f_xx, f_c2, f_gT, f_z1T, f_c) = more
        f_pg = sb("f_pg", [P, RING, TILES, 2])
        f_small = sb("f_small", [P, 24, TILES])
        f_stats = sb("f_stats", [P, 3, TILES, 6])
        f_mv = sb("f_mv", [P, 3, TILES, 2])
        f_SS = (f_S, f_c)
        seg_ring = sb("seg_ring", [P, RING, ROWS], BF16)
        f_seg_in = ring_sems("seg_in")
        F = {k: stage(k) for k in (
            "staged idx bn ag sd s1 t1 dv s_b tb nA nB TA TB zAT zBT scan U mU v z1 Tz1 z1T mR R m1 x1T m2 x2T "
            "Tx1 x1e Tx2 x2e m3 xx bn2 ag2 sd2 rs2 c2 y2 Tg gT mf feat mr sq sd3 nm rs3 h k1 k2 k3 k4").split()}
        f_pg_in, f_xs_in, f_xd_in = ring_sems("pg_in"), ring_sems("xs_in"), ring_sems("xd_in")
        f_xd_out, f_z1_out, f_r_out = ring_sems("xd_out"), ring_sems("z1_out"), ring_sems("r_out")
        f_t_out = {k: ring_sems(f"t{k}_out") for k in (1, 2, 3, 4)}

        def cols(b):
            return b[:, :, :].rearrange("p j d -> p (j d)")

        def tiles(b):
            return b.rearrange("p (j d) -> p j d", j=TILES)

        def edge_rows(table_ap, c, base=0):
            return table_ap[bass.ds(c.g * ROWS + base, ROWS), :].rearrange("(j p) d -> p j d", p=P)

        class Limit:

            made = 0

            def __init__(self, pool, array):
                below, self.register = (pool.alloc_register(f"limit_{Limit.made}_{i}") for i in range(2))
                Limit.made += 1
                pool.reg_mov(below, array.shape[0] - 2)
                self.set = lambda: pool.reg_add(self.register, below, 1)

        def gathers(pool, c, to, from_, limit, k, done):
            limit.set()
            for j in range(TILES):
                pool.indirect_dma_start(
                    out=to[:, c.s, j, :], out_offset=None, in_=from_,
                    in_offset=bass.IndirectOffsetOnAxis(ap=st_i[:, c.s, j, k:k + 1], axis=0),
                    bounds_check=limit.register, oob_is_err=False).then_inc(done[c.s], 16)

        ALL = 16 * TILES

        def first_pool(pool):
            limit = Limit(pool, x)

            def step(t):
                if c := t.at(1):
                    wait(pool, F["staged"], t.through(1))
                    wait(pool, F["dv"], t.through(1) - RING)
                    wait(pool, F["idx"], t.through(1) - RING)
                    gathers(pool, c, f_pg, node_table, limit, SRC, f_pg_in)
                    wait(pool, F["nA"], t.through(1) - RING)
                    wait(pool, f_xd_out[c.s], 16 * c.r)
                    gathers(pool, c, xd_ring, x, limit, DST, f_xd_in)
                    wait(pool, F["xx"], t.through(1) - RING)
                    gathers(pool, c, xs_ring, x, limit, SRC, f_xs_in)
            pipeline(pool, EG, 5, step)

        def load_segments(sp, c, k, done):
            sp.dma_start(seg_ring[:, c.s, :], segment_rows[k:k + 1, bass.ds(c.g * ROWS, ROWS)].broadcast_to([P, ROWS]))\
              .then_inc(done[c.s], 16)

        def first_sp(sp):
            def step(t):
                if c := t.at(1):
                    wait(sp, F["scan"], t.through(1) - RING)
                    load_segments(sp, c, 0, f_seg_in)
                if c := t.at(2):
                    wait(sp, f_xd_in[c.s], ALL * (c.r + 1))
                    sp.dma_start(edge_rows(x_dst, c), xd_ring[:, c.s, :, :]).then_inc(f_xd_out[c.s], 16)
                if c := t.at(4):
                    for k, r, done in ((1, t1b_ring, "x1e"), (2, t2b_ring, "x2e")):
                        wait(sp, F[done], t.through(4))
                        sp.dma_start(edge_rows(table[k], c, EP), r[:, c.s, :, :]).then_inc(f_t_out[k][c.s], 16)
                    wait(sp, F["z1"], t.through(4))
                    sp.dma_start(edge_rows(table[1], c), z1_ring[:, c.s, :, :]).then_inc(f_z1_out[c.s], 16)
                if c := t.at(5):
                    wait(sp, F["R"], t.through(5))
                    sp.dma_start(edge_rows(self_rows[0], c), r_ring[:, c.s, :, :]).then_inc(f_r_out[c.s], 16)
                    for k, r, done in ((3, t3b_ring, "feat"), (4, t4b_ring, "h")):
                        wait(sp, F[done], t.through(5))
                        sp.dma_start(edge_rows(table[k], c, EP), r[:, c.s, :, :]).then_inc(f_t_out[k][c.s], 16)
            pipeline(sp, EG, 5, step)
            for s in range(RING):
                for group in (f_xd_out, f_z1_out, f_r_out, *f_t_out.values()):
                    wait(sp, group[s], 16 * uses(EG, s))

        EQ, DV, T1, T2, SD, RS, SA, SB, TAm, TBm, SD2, RS2, SS, SD3, NM, RS3 = 0, 1, 2, 3, 4, 6, *range(8, 18)

        def first_dve(dve):
            def small(i, n=1):
                return f_small[:, i, :] if n == 1 else f_small[:, i:i + n, :]

            def step(t):
                if c := t.at(4):
                    wait(dve, F["rs2"], t.through(4))
                    wait(dve, F["c2"], t.before(4))
                    dve.tensor_tensor(f_c2[:, :, :], f_xx[:, :, :], per_row(f_mv[:, 2, :, 0]),
                                      ALU.subtract).then_inc(F["c2"], 1)
                    wait(dve, F["c2"], t.through(4))
                    wait(dve, F["Tg"], t.before(4))
                    dve.tensor_tensor(f_y2[:, :, :], f_c2[:, :, :], per_row(small(RS2)), ALU.mult).then_inc(F["y2"], 1)
                if c := t.at(2):
                    wait(dve, f_xd_in[c.s], ALL * (c.r + 1))
                    wait(dve, f_xs_in[c.s], ALL * (c.r + 1))
                    wait(dve, F["ag"], t.before(2))
                    for k, r in enumerate((xd_ring, xs_ring)):
                        for j in range(TILES):
                            last = dve.bn_stats(f_stats[:, k, j, :], r[:, c.s, j, :])
                    last.then_inc(F["bn"], 1)
                wait(dve, F["bn"], t.through(2))
                wait(dve, F["nB"], t.before(2))
                wait(dve, F["tb"], t.before(2))
                if c := t.at(2):
                    wait(dve, f_pg_in[c.s], ALL * (c.r + 1))
                    dve.tensor_scalar(small(EQ), f_pg[:, c.s, :, 1], 0.0, None, ALU.is_equal).then_inc(F["k1"], 1)
                    for k in range(2):
                        for j in range(TILES):
                            last = dve.bn_aggr(f_mv[:, k, j, :], f_stats[:, k, j, :])
                    last.then_inc(F["ag"], 1)
                    wait(dve, F["k1"], t.through(2))
                    dve.tensor_tensor(small(DV), small(EQ), f_pg[:, c.s, :, 1], ALU.add).then_inc(F["dv"], 1)
                    dve.tensor_tensor(small(T1), small(EQ), st_f[:, c.s, :, OWN], ALU.mult).then_inc(F["k2"], 1)
                    wait(dve, F["k2"], t.through(2))
                    dve.tensor_tensor(small(T2), small(T1), f_pg[:, c.s, :, 0], ALU.add).then_inc(F["k3"], 1)
                    wait(dve, F["k3"], t.through(2))
                    dve.tensor_copy(edge_i[:, bass.ds(c.g * TILES, TILES), TAB], small(T2)).then_inc(F["idx"], 1)
                if c := t.at(3):
                    wait(dve, F["zBT"], t.through(3))
                    wait(dve, f_seg_in[c.s], 16 * (c.r + 1))
                    wait(dve, F["scan"], t.before(3))
                    start = 0.0 if isinstance(c.g, int) and c.g == 0 else cols(f_SS[(c.s + 1) % 2])[:, ROWS - 1:ROWS]
                    dve.tensor_tensor_scan(cols(f_SS[c.s % 2]), seg_ring[:, c.s, :], cols(f_zBT), start,
                                           ALU.mult, ALU.add).then_inc(F["scan"], 1)
                    wait(dve, F["scan"], t.through(3))
                    wait(dve, F["mU"], t.before(3))
                    dve.tensor_tensor(f_U[:, :, :], f_SS[c.s % 2][:, :, :], f_zAT[:, :, :], ALU.add).then_inc(F["U"], 1)
                if c := t.at(2):
                    wait(dve, F["sd"], t.through(2))
                    dve.reciprocal(small(RS, 2), small(SD, 2)).then_inc(F["s1"], 1)
                    wait(dve, F["s1"], t.through(2))
                    wait(dve, F["nA"], t.before(2))
                    dve.tensor_tensor(small(SA), small(RS), st_f[:, c.s, :, DINV], ALU.mult)
                    dve.tensor_tensor(small(SB), small(RS + 1), small(DV), ALU.mult).then_inc(F["s_b"], 1)
                    wait(dve, F["s_b"], t.through(2))
                    dve.scalar_tensor_tensor(out=small(TAm), in0=f_mv[:, 0, :, 0], scalar=-1.0, in1=small(SA),
                                             op0=ALU.mult, op1=ALU.mult)
                    dve.scalar_tensor_tensor(out=small(TBm), in0=f_mv[:, 1, :, 0], scalar=-1.0, in1=small(SB),
                                             op0=ALU.mult, op1=ALU.mult).then_inc(F["tb"], 1)
                if c := t.at(3):
                    wait(dve, F["mU"], t.through(3))
                    wait(dve, F["z1"], t.before(3))
                    for j in range(TILES):
                        last = dve.scalar_tensor_tensor(out=f_v[:, j, :], in0=bank[5][:, j * P:(j + 1) * P],
                                                        scalar=st_f[:, c.s, j, DINV:DINV + 1], in1=bias_bc["gcn1"][:, :],
                                                        op0=ALU.mult, op1=ALU.add)
                    last.then_inc(F["v"], 1)
                    wait(dve, F["m3"], t.through(3))
                    wait(dve, F["c2"], t.before(3))
                    wait(dve, F["bn2"], t.before(3))
                    dve.scalar_tensor_tensor(out=cols(f_xx), in0=bank[1][:, :], scalar=0.0,
                                             in1=flat(xs_ring[:, c.s, :, :]), op0=ALU.max, op1=ALU.add).then_inc(F["xx"], 1)
                    wait(dve, F["xx"], t.through(3))
                    wait(dve, F["ag2"], t.before(3))
                    for j in range(TILES):
                        last = dve.bn_stats(f_stats[:, 2, j, :], f_xx[:, j, :])
                    last.then_inc(F["bn2"], 1)
                wait(dve, F["bn2"], t.through(3))
                if c := t.at(4):
                    wait(dve, F["sd3"], t.through(4))
                    dve.tensor_scalar(small(NM), small(SD3), NORM_EPS, None, ALU.max).then_inc(F["nm"], 1)
                if c := t.at(3):
                    for j in range(TILES):
                        last = dve.bn_aggr(f_mv[:, 2, j, :], f_stats[:, 2, j, :])
                    last.then_inc(F["ag2"], 1)
                if c := t.at(4):
                    wait(dve, F["nm"], t.through(4))
                    wait(dve, F["h"], t.before(4))
                    dve.reciprocal(small(RS3), small(NM)).then_inc(F["rs3"], 1)
                    wait(dve, F["mR"], t.through(4))
                    wait(dve, f_r_out[c.s], 16 * c.r)
                    for j in range(TILES):
                        last = dve.scalar_tensor_tensor(out=r_ring[:, c.s, j, :], in0=bank[6][:, j * P:(j + 1) * P],
                                                        scalar=st_f[:, c.s, j, DINV:DINV + 1], in1=bias_bc["gcn2"][:, :],
                                                        op0=ALU.mult, op1=ALU.add)
                    last.then_inc(F["R"], 1)
                if c := t.at(3):
                    wait(dve, F["sd2"], t.through(3))
                    wait(dve, F["y2"], t.before(3))
                    dve.reciprocal(small(RS2), small(SD2)).then_inc(F["rs2"], 1)
                if c := t.at(0):
                    wait(dve, F["z1"], t.through(0) - RING)
                    wait(dve, F["R"], t.through(0) - RING)
                    for own in (f_pg_in, f_xs_in, f_xd_in):
                        wait(dve, own[c.s], ALL * c.r)
                    dve.tensor_copy(st_i[:, c.s, :, :], group_of(edge_i, c))
                    dve.tensor_copy(st_f[:, c.s, :, :], group_of(edge_f, c)).then_inc(F["staged"], 1)
            pipeline(dve, EG, 5, step)

        def first_act(act):
            def small(i, n=1):
                return f_small[:, i, :] if n == 1 else f_small[:, i:i + n, :]

            def step(t):
                if c := t.at(3):
                    wait(act, F["m1"], t.through(3))
                    wait(act, F["m2"], t.before(3))
                    act.activation(cols(f_x1T), bank[0][:, :], ACT.Relu, bias=bias_col[:, 0:1]).then_inc(F["x1T"], 1)
                if c := t.at(4):
                    wait(act, F["Tz1"], t.through(4))
                    wait(act, F["mR"], t.before(4))
                    act.activation(cols(f_z1T), bank[1][:, :], ACT.Copy).then_inc(F["z1T"], 1)
                if c := t.at(3):
                    wait(act, F["Tx1"], t.through(3))
                    wait(act, f_t_out[1][c.s], 16 * c.r)
                    act.activation(flat(t1b_ring[:, c.s, :, :]), bank[2][:, :], ACT.Copy).then_inc(F["x1e"], 1)
                    wait(act, F["m2"], t.through(3))
                    wait(act, F["m3"], t.before(3))
                    act.activation(cols(f_x2T), bank[3][:, :], ACT.Relu, bias=bias_col[:, 1:2]).then_inc(F["x2T"], 1)
                if c := t.at(4):
                    wait(act, F["Tg"], t.through(4))
                    wait(act, F["mr"], t.before(4))
                    act.activation(cols(f_gT), bank[4][:, :], ACT.Relu).then_inc(F["gT"], 1)
                if c := t.at(3):
                    wait(act, F["Tx2"], t.through(3))
                    wait(act, f_t_out[2][c.s], 16 * c.r)
                    act.activation(flat(t2b_ring[:, c.s, :, :]), bank[0][:, :], ACT.Copy).then_inc(F["x2e"], 1)
                if c := t.at(2):
                    wait(act, F["ag"], t.through(2))
                    wait(act, F["s1"], t.before(2))
                    act.activation(small(SD, 2), f_mv[:, 0:2, :, 1], ACT.Sqrt, bias=eps_col[:, 0:1]).then_inc(F["sd"], 1)
                if c := t.at(4):
                    wait(act, F["mf"], t.through(4))
                    wait(act, f_t_out[3][c.s], 16 * c.r)
                    act.activation(flat(t3b_ring[:, c.s, :, :]), bank[4][:, :], ACT.Relu).then_inc(F["feat"], 1)
                    wait(act, F["mr"], t.through(4))
                    wait(act, F["sd3"], t.before(4))
                    for j in range(TILES):
                        last = act.activation(junk[:, j, :], bank[7][:, j * P:(j + 1) * P], ACT.Square,
                                              accum_out=small(SS)[:, j:j + 1])
                    last.then_inc(F["sq"], 1)
                    wait(act, F["sq"], t.through(4))
                    wait(act, F["nm"], t.before(4))
                    act.activation(small(SD3), small(SS), ACT.Sqrt).then_inc(F["sd3"], 1)
                if c := t.at(3):
                    wait(act, F["v"], t.through(3))
                    wait(act, f_z1_out[c.s], 16 * c.r)
                    wait(act, F["Tz1"], t.through(3) - RING)
                    for j in range(TILES):
                        last = act.activation(z1_ring[:, c.s, j, :], f_v[:, j, :], ACT.Relu,
                                              scale=st_f[:, c.s, j, DINV:DINV + 1])
                    last.then_inc(F["z1"], 1)
                if c := t.at(2):
                    wait(act, F["tb"], t.through(2))
                    wait(act, F["TA"], t.before(2))
                    for j in range(TILES):
                        last = act.activation(f_zA[:, j, :], xd_ring[:, c.s, j, :], ACT.Relu,
                                              scale=small(SA)[:, j:j + 1], bias=small(TAm)[:, j:j + 1])
                    last.then_inc(F["nA"], 1)
                    wait(act, F["TB"], t.before(2))
                    for j in range(TILES):
                        last = act.activation(f_zB[:, j, :], xs_ring[:, c.s, j, :], ACT.Relu,
                                              scale=small(SB)[:, j:j + 1], bias=small(TBm)[:, j:j + 1])
                    last.then_inc(F["nB"], 1)
                if c := t.at(3):
                    wait(act, F["ag2"], t.through(3))
                    wait(act, F["rs2"], t.before(3))
                    act.activation(small(SD2), f_mv[:, 2, :, 1], ACT.Sqrt, bias=eps_col[:, 0:1]).then_inc(F["sd2"], 1)
                if c := t.at(4):
                    wait(act, F["rs3"], t.through(4))
                    wait(act, f_t_out[4][c.s], 16 * c.r)
                    for j in range(TILES):
                        last = act.activation(t4b_ring[:, c.s, j, :], bank[7][:, j * P:(j + 1) * P], ACT.Relu,
                                              scale=small(RS3)[:, j:j + 1])
                    last.then_inc(F["h"], 1)
                if c := t.at(2):
                    wait(act, F["TA"], t.through(2))
                    wait(act, F["U"], t.before(2))
                    act.activation(cols(f_zAT), bank[3][:, :], ACT.Copy).then_inc(F["zAT"], 1)
                    wait(act, F["TB"], t.through(2))
                    wait(act, F["m1"], t.before(2))
                    wait(act, F["scan"], t.before(2))
                    act.activation(cols(f_zBT), bank[2][:, :], ACT.Copy).then_inc(F["zBT"], 1)
            pipeline(act, EG, 5, step)

        def transposes(pe, to, rows, done):
            for j in range(TILES):
                last = pe.transpose(bank[to][:, j * P:(j + 1) * P], rows[:, j, :], ident[:, :])
            last.then_inc(done, 1)

        def rows_matmul(pe, to, columns, w, bias, done):
            if bias is not None:
                pe.matmul(bank[to][:, :], ones3[:, :],
                          bias3[:, ROW_BIASES.index(bias), :, :].rearrange("k j d -> k (j d)"),
                          start=True, stop=False)
            for j in range(TILES):
                last = pe.matmul(bank[to][:, j * P:(j + 1) * P], columns[:, j * P:(j + 1) * P], w_sb[w][:, :],
                                 start=bias is None, stop=bias is None or j == TILES - 1)
            last.then_inc(done, 1)

        def first_pe(pe):
            def step(t):
                if c := t.at(3):
                    wait(pe, F["zBT"], t.through(3))
                    wait(pe, F["x2e"], t.before(3))
                    pe.matmul(bank[0][:, :], w_sb["gcn1"][:, :], cols(f_zBT), start=True, stop=True).then_inc(F["m1"], 1)
                if c := t.at(4):
                    wait(pe, F["z1"], t.through(4))
                    wait(pe, F["xx"], t.before(3))
                    transposes(pe, 1, z1_ring[:, c.s, :, :], F["Tz1"])
                    wait(pe, F["y2"], t.through(4))
                    wait(pe, F["feat"], t.before(4))
                    transposes(pe, 4, f_y2, F["Tg"])
                if c := t.at(3):
                    wait(pe, F["x1T"], t.through(3))
                    wait(pe, F["zBT"], t.through(3))
                    transposes(pe, 2, f_x1T, F["Tx1"])
                    wait(pe, F["zAT"], t.through(3))
                    pe.matmul(bank[3][:, :], w_sb["gcn2"][:, :], cols(f_x1T), start=True, stop=True).then_inc(F["m2"], 1)
                    wait(pe, F["U"], t.through(3))
                    wait(pe, F["v"], t.before(3))
                    rows_matmul(pe, 5, cols(f_U), "gcn1", None, F["mU"])
                if c := t.at(4):
                    wait(pe, F["z1T"], t.through(4))
                    wait(pe, F["R"], t.before(4))
                    rows_matmul(pe, 6, cols(f_z1T), "gcn2", None, F["mR"])
                if c := t.at(3):
                    wait(pe, F["x2T"], t.through(3))
                    transposes(pe, 0, f_x2T, F["Tx2"])
                wait(pe, F["z1T"], t.through(4))
                if c := t.at(3):
                    rows_matmul(pe, 1, cols(f_x2T), "gcn3", "gcn3", F["m3"])
                if c := t.at(4):
                    wait(pe, F["gT"], t.through(4))
                    rows_matmul(pe, 4, cols(f_gT), "pool", "pool", F["mf"])
                    wait(pe, F["h"], t.before(4))
                    rows_matmul(pe, 7, cols(f_gT), "self1", "one", F["mr"])
                wait(pe, F["x1e"], t.through(3))
                wait(pe, F["x2T"], t.through(3))
                if c := t.at(2):
                    wait(pe, F["nA"], t.through(2))
                    transposes(pe, 3, f_zA, F["TA"])
                    wait(pe, F["nB"], t.through(2))
                    transposes(pe, 2, f_zB, F["TB"])
            pipeline(pe, EG, 5, step)

        g_ring, self_ring, more_ring, msg_ring, self_out_ring, xx_out_ring = ring[0:6]
        d_w, d_S0, d_S1, d_v, d_n, d_nT = buf[0:6]
        d_S = (d_S0, d_S1)
        STAGES = {
            1: "staged TB scan mU v msg Tg gT mf fin",
            2: "staged TB scan mU v xx bn ag sd s1 tb y2 Tg gT mf mr msg fin",
            3: "staged w TB scan mU v sq sd nm s1 msg Tg gT mf fin",
            4: "staged w TB scan mU v fin",
        }
        RINGS = {1: "gathered seg self out1 out2", 2: "gathered seg self more out1 out2 out3",
                 3: "gathered seg self out1 out2", 4: "gathered seg self more scattered"}
        D = {k: stage(k) for k in dict.fromkeys(" ".join(STAGES.values()).split())}
        DR = {"gathered": f_xs_in, "seg": f_seg_in, "self": ring_sems("r_in"), "more": ring_sems("more_in"),
              "out1": f_z1_out, "out2": f_r_out, "out3": f_xd_out, "scattered": t_scattered}
        TAKES = {1: "gcn2", 2: "gcn3", 3: "neigh1", 4: "neigh2"}
        SCALE = {1: DINV, 2: DINV, 3: CINV, 4: CD}

        class Round:
            def __init__(self, k):
                self.k = k

            def wait(self, engine, name, groups):
                wait(engine, D[name], groups)

            def ring_wait(self, engine, name, c, more=0):
                each = 16 * TILES if name in ("gathered", "scattered") else 16
                wait(engine, DR[name][c.s], (c.r + more) * each)

            def all_done(self, engine, name):
                for s in range(RING):
                    self.ring_wait(engine, name, Turn(s, uses(EG, s), s))

        def round_sp(sp, k):
            r = Round(k)

            def load(c, name, to, from_):
                sp.dma_start(to[:, c.s, :, :], edge_rows(from_, c)).then_inc(DR[name][c.s], 16)

            def store(c, name, to, from_):
                sp.dma_start(edge_rows(to, c), from_[:, c.s, :, :]).then_inc(DR[name][c.s], 16)

            def step(t):
                if c := t.at(1):
                    r.wait(sp, "scan", t.through(1) - RING)
                    load_segments(sp, c, 1 if k == 3 else 0, DR["seg"])
                    r.wait(sp, "v", t.through(1) - RING)
                    load(c, "self", self_ring, self_rows[(k + 1) % 2])
                    if k in (2, 4):
                        r.wait(sp, "xx" if k == 2 else "fin", t.through(1) - RING)
                        load(c, "more", more_ring, x_dst if k == 2 else xx_dst)
                if c := t.at(5):
                    if k < 4:
                        r.wait(sp, "msg", t.through(5))
                        store(c, "out1", table[k + 1], msg_ring)
                        if k == 2:
                            store(c, "out3", xx_dst, xx_out_ring)
                        r.wait(sp, "fin", t.through(5))
                        store(c, "out2", self_rows[k % 2], self_out_ring)
            pipeline(sp, EG, 5, step)
            for name in ("out1", "out2", "out3"):
                if name in RINGS[k].split():
                    r.all_done(sp, name)

        def round_pool(pool, k):
            r = Round(k)
            table_limit = Limit(pool, table[k])
            out_limit = Limit(pool, out)

            def step(t):
                if k == 4 and (c := t.at(4)):
                    r.wait(pool, "fin", t.through(4))
                    out_limit.set()
                    for j in range(TILES):
                        pool.indirect_dma_start(
                            out=out, out_offset=bass.IndirectOffsetOnAxis(ap=st_i[:, c.s, j, SCAT:SCAT + 1], axis=0),
                            in_=self_out_ring[:, c.s, j, :], in_offset=None, bounds_check=out_limit.register,
                            oob_is_err=False).then_inc(DR["scattered"][c.s], 16)
                if c := t.at(1):
                    r.wait(pool, "staged", t.through(1))
                    r.wait(pool, "w" if k >= 3 else "TB", t.through(1) - RING)
                    gathers(pool, c, g_ring, table[k], table_limit, TAB, DR["gathered"])
            pipeline(pool, EG, 5, step)
            if k == 4:
                r.all_done(pool, "scattered")

        D_SD, D_RS, D_TB, D_SS, D_NM = range(5)

        def round_dve(dve, k):
            r = Round(k)

            def scaled(c, to, from_bank, factor, plus):
                for j in range(TILES):
                    last = dve.scalar_tensor_tensor(out=to[:, j, :], in0=bank[from_bank][:, j * P:(j + 1) * P],
                                                    scalar=st_f[:, c.s, j, factor:factor + 1], in1=plus(j),
                                                    op0=ALU.mult, op1=ALU.add)
                return last

            def step(t):
                if k >= 3 and (c := t.at(2)):
                    r.ring_wait(dve, "gathered", c, 1)
                    r.wait(dve, "TB", t.before(2))
                    dve.tensor_tensor(d_w[:, :, :], g_ring[:, c.s, :, :], per_row(st_f[:, c.s, :, WEIGHT]),
                                      ALU.mult).then_inc(D["w"], 1)
                if c := t.at(3):
                    r.wait(dve, "mU", t.through(3))
                    r.ring_wait(dve, "self", c, 1)
                    if k in (1, 3):
                        r.wait(dve, "msg", t.before(3))
                    scaled(c, d_v, 1, SCALE[k], lambda j: self_ring[:, c.s, j, :]).then_inc(D["v"], 1)
                    if k == 2:
                        r.wait(dve, "v", t.through(3))
                        r.ring_wait(dve, "more", c, 1)
                        r.ring_wait(dve, "out3", c)
                        r.wait(dve, "y2", t.through(3) - RING)
                        dve.scalar_tensor_tensor(out=flat(xx_out_ring[:, c.s, :, :]), in0=cols(d_v), scalar=0.0,
                                                 in1=flat(more_ring[:, c.s, :, :]), op0=ALU.max,
                                                 op1=ALU.add).then_inc(D["xx"], 1)
                        r.wait(dve, "xx", t.through(3))
                        r.wait(dve, "ag", t.before(3))
                        for j in range(TILES):
                            last = dve.bn_stats(f_stats[:, 0, j, :], xx_out_ring[:, c.s, j, :])
                        last.then_inc(D["bn"], 1)
                    if k == 4:
                        r.wait(dve, "v", t.through(3))
                        r.ring_wait(dve, "more", c, 1)
                        r.ring_wait(dve, "scattered", c)
                        dve.scalar_tensor_tensor(out=flat(self_out_ring[:, c.s, :, :]), in0=cols(d_v), scalar=0.0,
                                                 in1=flat(more_ring[:, c.s, :, :]), op0=ALU.max,
                                                 op1=ALU.add).then_inc(D["fin"], 1)
                if k == 2:
                    r.wait(dve, "bn", t.through(3))
                    r.wait(dve, "sd", t.before(3))
                    r.wait(dve, "tb", t.before(3))
                if c := t.at(2):
                    r.wait(dve, "TB", t.through(2))
                    r.ring_wait(dve, "seg", c, 1)
                    r.wait(dve, "mU", t.before(2) - 1)
                    r.wait(dve, "scan", t.before(2))
                    first = isinstance(c.g, int) and c.g == 0
                    start = 0.0 if first else cols(d_S[(c.s + 1) % 2])[:, ROWS - 1:ROWS]
                    ops = (ALU.add, ALU.max) if k == 3 else (ALU.mult, ALU.add)
                    dve.tensor_tensor_scan(cols(d_S[c.s % 2]), seg_ring[:, c.s, :], bank[0][:, :], start, *ops)\
                       .then_inc(D["scan"], 1)
                if k == 2 and (c := t.at(3)):
                    for j in range(TILES):
                        last = dve.bn_aggr(f_mv[:, 0, j, :], f_stats[:, 0, j, :])
                    last.then_inc(D["ag"], 1)
                if k == 1 and (c := t.at(4)):
                    r.wait(dve, "mf", t.through(4))
                    r.ring_wait(dve, "out2", c)
                    plus = bias_bc["gcn3"]
                    scaled(c, self_out_ring[:, c.s, :, :], 3, DINV, lambda j: plus[:, :]).then_inc(D["fin"], 1)
                if k == 2 and (c := t.at(3)):
                    r.wait(dve, "sd", t.through(3))
                    r.wait(dve, "y2", t.before(3))
                    dve.reciprocal(f_small[:, D_RS, :], f_small[:, D_SD, :]).then_inc(D["s1"], 1)
                    r.wait(dve, "s1", t.through(3))
                    dve.scalar_tensor_tensor(out=f_small[:, D_TB, :], in0=f_mv[:, 0, :, 0], scalar=-1.0,
                                             in1=f_small[:, D_RS, :], op0=ALU.mult, op1=ALU.mult).then_inc(D["tb"], 1)
                if k == 3 and (c := t.at(3)):
                    r.wait(dve, "sd", t.through(3))
                    dve.tensor_scalar(f_small[:, D_NM, :], f_small[:, D_SD, :], NORM_EPS, None, ALU.max)\
                       .then_inc(D["nm"], 1)
                    r.wait(dve, "nm", t.through(3))
                    dve.reciprocal(f_small[:, D_RS, :], f_small[:, D_NM, :]).then_inc(D["s1"], 1)
                if c := t.at(0):
                    r.ring_wait(dve, "gathered", c)
                    for user in {1: ("v", "msg", "fin"), 2: ("v",), 3: ("w", "v"), 4: ("w", "v")}[k]:
                        r.wait(dve, user, t.through(0) - RING)
                    if k == 4:
                        r.ring_wait(dve, "scattered", c)
                    dve.tensor_copy(st_i[:, c.s, :, :], group_of(edge_i, c))
                    dve.tensor_copy(st_f[:, c.s, :, :], group_of(edge_f, c)).then_inc(D["staged"], 1)
            pipeline(dve, EG, 5, step)

        def round_act(act, k):
            r = Round(k)

            def step(t):
                if k == 2 and (c := t.at(4)):
                    r.wait(act, "tb", t.through(4))
                    r.wait(act, "Tg", t.before(4))
                    for j in range(TILES):
                        last = act.activation(d_n[:, j, :], xx_out_ring[:, c.s, j, :], ACT.Relu,
                                              scale=f_small[:, D_RS, j:j + 1], bias=f_small[:, D_TB, j:j + 1])
                    last.then_inc(D["y2"], 1)
                if k == 3 and (c := t.at(4)):
                    r.wait(act, "s1", t.through(4))
                    r.ring_wait(act, "out1", c)
                    r.wait(act, "Tg", t.through(4) - RING)
                    for j in range(TILES):
                        last = act.activation(msg_ring[:, c.s, j, :], d_v[:, j, :], ACT.Relu,
                                              scale=f_small[:, D_RS, j:j + 1])
                    last.then_inc(D["msg"], 1)
                if k < 4 and (c := t.at(4)):
                    r.wait(act, "Tg", t.through(4))
                    r.wait(act, "mr" if k == 2 else "mf", t.before(4))
                    act.activation(cols(d_nT), bank[2][:, :], ACT.Copy).then_inc(D["gT"], 1)
                if k == 1 and (c := t.at(3)):
                    r.wait(act, "v", t.through(3))
                    r.ring_wait(act, "out1", c)
                    r.wait(act, "Tg", t.through(3) - RING)
                    for j in range(TILES):
                        last = act.activation(msg_ring[:, c.s, j, :], d_v[:, j, :], ACT.Relu,
                                              scale=st_f[:, c.s, j, DINV:DINV + 1])
                    last.then_inc(D["msg"], 1)
                if k == 2 and (c := t.at(4)):
                    r.wait(act, "mf", t.through(4))
                    r.ring_wait(act, "out1", c)
                    act.activation(flat(msg_ring[:, c.s, :, :]), bank[3][:, :], ACT.Relu).then_inc(D["msg"], 1)
                    r.wait(act, "mr", t.through(4))
                    r.ring_wait(act, "out2", c)
                    act.activation(flat(self_out_ring[:, c.s, :, :]), bank[4][:, :], ACT.Copy).then_inc(D["fin"], 1)
                if k == 3 and (c := t.at(4)):
                    r.wait(act, "mf", t.through(4))
                    r.ring_wait(act, "out2", c)
                    act.activation(flat(self_out_ring[:, c.s, :, :]), bank[3][:, :], ACT.Copy).then_inc(D["fin"], 1)
                if k == 2 and (c := t.at(3)):
                    r.wait(act, "ag", t.through(3))
                    r.wait(act, "s1", t.before(3))
                    act.activation(f_small[:, D_SD, :], f_mv[:, 0, :, 1], ACT.Sqrt,
                                   bias=eps_col[:, 0:1]).then_inc(D["sd"], 1)
                if k == 3 and (c := t.at(3)):
                    r.wait(act, "v", t.through(3))
                    r.wait(act, "sd", t.before(3))
                    for j in range(TILES):
                        last = act.activation(junk[:, j, :], d_v[:, j, :], ACT.Square,
                                              accum_out=f_small[:, D_SS, j:j + 1])
                    last.then_inc(D["sq"], 1)
                    r.wait(act, "sq", t.through(3))
                    r.wait(act, "nm", t.before(3))
                    act.activation(f_small[:, D_SD, :], f_small[:, D_SS, :], ACT.Sqrt).then_inc(D["sd"], 1)
            if k < 4:
                pipeline(act, EG, 5, step)

        def round_pe(pe, k):
            r = Round(k)

            def step(t):
                if c := t.at(3):
                    r.wait(pe, "scan", t.through(3))
                    r.wait(pe, "v", t.before(3))
                    rows_matmul(pe, 1, cols(d_S[c.s % 2]), TAKES[k], None, D["mU"])
                if c := t.at(2):
                    if k >= 3:
                        r.wait(pe, "w", t.through(2))
                    else:
                        r.ring_wait(pe, "gathered", c, 1)
                    r.wait(pe, "scan", t.before(2))
                    transposes(pe, 0, d_w if k >= 3 else g_ring[:, c.s, :, :], D["TB"])
                if k < 4 and (c := t.at(4)):
                    r.wait(pe, "y2" if k == 2 else "msg", t.through(4))
                    r.wait(pe, "gT", t.before(4))
                    transposes(pe, 2, d_n if k == 2 else msg_ring[:, c.s, :, :], D["Tg"])
                    r.wait(pe, "gT", t.through(4))
                    if k == 1:
                        r.wait(pe, "fin", t.before(4))
                        rows_matmul(pe, 3, cols(d_nT), "gcn3", None, D["mf"])
                    if k == 2:
                        r.wait(pe, "msg", t.before(4))
                        rows_matmul(pe, 3, cols(d_nT), "pool", "pool", D["mf"])
                        r.wait(pe, "fin", t.before(4))
                        rows_matmul(pe, 4, cols(d_nT), "self1", "one", D["mr"])
                    if k == 3:
                        r.wait(pe, "fin", t.before(4))
                        rows_matmul(pe, 3, cols(d_nT), "self2", "two", D["mf"])
            pipeline(pe, EG, 5, step)

        def phase(sp=None, pool=None, dve=None, act=None, pe=None, k=None):
            args = () if k is None else (k,)
            with nc.Block() as block:
                if sp:
                    @block.sync
                    def _(engine):
                        sp(engine, *args)
                if pool:
                    @block.gpsimd
                    def _(engine):
                        pool(engine, *args)
                if dve:
                    @block.vector
                    def _(engine):
                        dve(engine, *args)
                if act:
                    @block.scalar
                    def _(engine):
                        act(engine, *args)
                if pe:
                    @block.tensor
                    def _(engine):
                        pe(engine, *args)

        def const_sp(sp):
            for k, name in enumerate(("gcn1", "gcn2")):
                sp.dma_start(bias_col[:, k:k + 1], B[name].rearrange("(p a) -> p a", a=1)).then_inc(bias_in, 16)
            for k, name in enumerate(ROW_BIASES):
                sp.dma_start(bias_row[:, k, :], B[name].rearrange("(a n) -> a n", a=1)).then_inc(bias_in, 16)
            for k in bias_bc:
                sp.dma_start(bias_bc[k][:, :], B[k].rearrange("(a n) -> a n", a=1).broadcast_to([P, P]))\
                  .then_inc(bias_bc_in, 16)
            for k in W:
                sp.dma_start(w_sb[k][:, :], W[k]).then_inc(w_in, 16)
            sp.wait_ge(bias_split, BIAS_SPLIT_ALL)
            for k in range(3):
                for j in range(TILES):
                    sp.dma_start(bias3[k:k + 1, :, j, :], bias_part[k][:, :, :]).then_inc(bias3_in, 16)
            sp.wait_ge(bias_in, 16 * (2 + len(ROW_BIASES)))
            sp.wait_ge(bias_bc_in, 16 * len(bias_bc))
            sp.wait_ge(w_in, 16 * len(W))
            sp.wait_ge(bias3_in, 16 * 3 * TILES)

        def const_pool(pool):
            pool.memset(ones3[:, :], 1.0).then_inc(ones3_done, 1)
            pool.memset(ident[:, :], 0.0).then_inc(zeros_done, 1)
            pool.wait_ge(zeros_done, 1)
            pool.affine_select(out=ident[:, :], in_=ident[:, :], compare_op=ALU.not_equal, fill=1.0, base=0,
                               pattern=[[-1, P]], channel_multiplier=1).then_inc(ident_done, 1)

        ONE, FOUR = 16, 16 * TILES
        phase(const_sp, const_pool, const_dve)
        phase(prep_sp, prep_pool, prep_dve, prep_act, prep_pe)
        phase(None, table_pool, table_dve)
        passed(EG, ["staged"], {"scattered": FOUR})
        phase(first_sp, first_pool, first_dve, first_act, first_pe)
        passed(EG, F, {"pg_in": FOUR, "xs_in": FOUR, "xd_in": FOUR, "seg_in": ONE, "xd_out": ONE, "z1_out": ONE,
                       "r_out": ONE, **{f"t{k}_out": ONE for k in (1, 2, 3, 4)}})
        IN_RINGS = {"gathered": ("xs_in", FOUR), "seg": ("seg_in", ONE), "self": ("r_in", ONE), "more": ("more_in", ONE),
                    "out1": ("z1_out", ONE), "out2": ("r_out", ONE), "out3": ("xd_out", ONE)}
        for k in (1, 2, 3):
            phase(round_sp, round_pool, round_dve, round_act, round_pe, k)
            passed(EG, STAGES[k].split(), dict(IN_RINGS[name] for name in RINGS[k].split()))
        phase(node_sp, node_pool, node_dve, node_act, node_pe)
        passed(NG, S, {"loaded": ONE, "stored": ONE})
        phase(round_sp, round_pool, round_dve, None, round_pe, 4)


_W = {"gcn1": "L0_gnn_W1", "gcn2": "L0_gnn_W2", "gcn3": "L0_gnn_W3", "pool": "L1_gnn_W_pool",
      "self1": "L1_gnn_W1_self", "neigh1": "L1_gnn_W1_neigh", "self2": "L1_gnn_W2_self", "neigh2": "L1_gnn_W2_neigh"}
_B = {"gcn1": "L0_gnn_b1", "gcn2": "L0_gnn_b2", "gcn3": "L0_gnn_b3", "pool": "L1_gnn_b_pool",
      "one": "L1_gnn_b1", "two": "L1_gnn_b2"}


def kernel(**inputs):
    import numpy as _np
    import concourse.bacc as _bacc
    from concourse.bass_utils import run_bass_kernel_spmd as _run

    nc = _bacc.Bacc("TRN2", target_bir_lowering=False, num_devices=1)
    arrays, aps = {}, {}
    for name in ["x", "src", "dst", "edge_weight", *_W.values(), *_B.values()]:
        a = _np.ascontiguousarray(inputs[name])
        arrays[name] = a
        aps[name] = nc.dram_tensor(name, a.shape, mybir.dt.from_np(a.dtype), kind="ExternalInput").ap()
    out = nc.dram_tensor("out", inputs["x"].shape, F32, kind="ExternalOutput").ap()
    gnn_kernel(nc, aps["x"], aps["src"], aps["dst"], aps["edge_weight"],
               {k: aps[v] for k, v in _W.items()}, {k: aps[v] for k, v in _B.items()}, out)
    r = _run(nc, [arrays], core_ids=[0])
    return r.results[0]["out"]
```

```python
import numpy as np
import concourse.bass as bass
from concourse import mybir
from contextlib import ExitStack

F32 = mybir.dt.float32
BF16 = mybir.dt.bfloat16
I32 = mybir.dt.int32
U32 = mybir.dt.uint32
ALU = mybir.AluOpType
ACT = mybir.ActivationFunctionType

P = 128
TILES = 4
ROWS = P * TILES
RING = 4
LN_EPS = 1e-5
NORM_EPS = 1e-12
FAR = 3.0e38


class Turn:

    def __init__(self, g, r, s):
        self.g, self.r, self.s = g, r, s


class Step:

    def __init__(self, i, u, n, shift=0):
        if isinstance(i, int):
            i, shift = i + shift, 0
        self.i, self.u, self.n = i, u + RING * shift, n

    def _plus(self, c):
        v = RING * self.i + c
        return min(max(v, 0), self.n) if isinstance(self.i, int) else v

    def at(self, lag):
        c = self.u - lag
        if isinstance(self.i, int):
            g = RING * self.i + c
            return Turn(g, g // RING, g % RING) if 0 <= g < self.n else None
        return Turn(RING * self.i + c, self.i + c // RING, c % RING)

    def through(self, lag):
        return self._plus(self.u - lag + 1)

    def before(self, lag):
        return self._plus(self.u - lag)


class Part:

    def __init__(self, n, last_lag, shift=0):
        self.n, self.last_lag, self.shift = n, last_lag, shift

    def kind(self, q):
        own = q + self.shift
        if own < 0 or own * RING >= self.n + self.last_lag:
            return "off"
        return "full" if -(-self.last_lag // RING) + 1 <= own < (self.n - 1) // RING else "edge"

    def step(self, i, u):
        return Step(i, u, self.n, self.shift)


def run(engine, quads, work):

    def quad(q, i):
        for u in range(RING):
            for part, does in work:
                if part.kind(q) == "full" or (part.kind(q) == "edge" and
                                              RING * (q + part.shift) + u < part.n + part.last_lag):
                    does(part.step(i, u))

    q = 0
    while q < quads:
        kinds = [part.kind(q) for part, _ in work]
        end = q + 1
        while "edge" not in kinds and end < quads and [part.kind(end) for part, _ in work] == kinds:
            end += 1
        if end - q > 1:
            with engine.Fori(q, end) as i:
                quad(q, i)
        else:
            quad(q, q)
        q = end


def pipeline(engine, n, last_lag, step):
    run(engine, -(-(n + last_lag) // RING), [(Part(n, last_lag), step)])




def gnn_kernel(nc, x, src, dst, edge_weight, W, B, out):
    N, D = x.shape
    E = src.shape[0]
    assert D == P
    NODE_GROUPS = -(-N // ROWS)

    ctx = ExitStack()
    with ctx:
        def sb(name, shape, dt=F32):
            return ctx.enter_context(nc.sbuf_tensor(name, shape, dt))

        def sem(name):
            return ctx.enter_context(nc.semaphore(name))

        def flat(t):
            return t.rearrange("p j d -> p (j d)")

        def per_row(col):
            return col.unsqueeze(2).broadcast_to([P, TILES, P])

        stages, ring_places, started = {}, {}, {}

        def stage(name):
            if name not in stages:
                stages[name] = sem(f"done_{name}")
            return stages[name]

        def ring_sems(name):
            if name not in ring_places:
                ring_places[name] = [sem(f"{name}_{s}") for s in range(RING)]
            return ring_places[name]

        def due(semaphore, groups):
            if isinstance(groups, int) and groups <= 0:
                return None
            return groups + started.get(semaphore.name, 0)

        def uses(n, s):
            return len(range(s, n, RING))

        def passed(n, names, rings):
            for name in names:
                k = stages[name].name
                started[k] = started.get(k, 0) + n
            for name, each in rings.items():
                for s in range(RING):
                    k = ring_places[name][s].name
                    started[k] = started.get(k, 0) + each * uses(n, s)

        ring = [sb(f"ring{i}", [P, RING, TILES, P]) for i in range(9)]
        buf = [sb(f"buf{i}", [P, TILES, P]) for i in range(17)]
        junk = sb("junk", [P, TILES, P])
        bank = [ctx.enter_context(nc.psum_tensor(f"bank{i}", [P, ROWS], F32)) for i in range(8)]

        w_sb = {k: sb(f"w_{k}", [P, P]) for k in W}
        w_in = sem("w_in")
        ident = sb("ident", [P, P])
        zeros_done, ident_done, ones3_done = sem("zeros_done"), sem("ident_done"), sem("ones3_done")
        ones3 = sb("ones3", [3, P], BF16)
        ones_col = sb("ones_col", [P, 1])
        ones_col_done = sem("ones_col_done")
        bias_col = sb("bias_col", [P, 3])
        bias_in = sem("bias_in")
        ROW_BIASES = ("gcn3", "pool", "one", "two")
        bias_row = sb("bias_row", [1, len(ROW_BIASES), P])
        bias_rest = sb("bias_rest", [1, 2, len(ROW_BIASES), P])
        bias_part = [sb(f"bias_part{k}", [1, len(ROW_BIASES), P], BF16) for k in range(3)]
        bias3 = sb("bias3", [3, len(ROW_BIASES), TILES, P], BF16)
        bias_split, bias3_in = sem("bias_split"), sem("bias3_in")
        eps_col = sb("eps_col", [P, 1])
        eps_done = sem("eps_done")

        def const_dve(dve):
            dve.memset(eps_col[:, :], LN_EPS).then_inc(eps_done, 1)
            dve.wait_ge(bias_in, 16 * (3 + len(ROW_BIASES)))
            n = 0
            rest = bias_row[:, :, :]
            for k in range(3):
                dve.tensor_copy(bias_part[k][:, :, :], rest).then_inc(bias_split, 1)
                n += 1
                if k < 2:
                    dve.wait_ge(bias_split, n)
                    dve.tensor_tensor(bias_rest[:, k, :, :], rest, bias_part[k][:, :, :],
                                      ALU.subtract).then_inc(bias_split, 1)
                    n += 1
                    dve.wait_ge(bias_split, n)
                    rest = bias_rest[:, k, :, :]

        BIAS_SPLIT_ALL = 5

        NG = NODE_GROUPS
        x_ring, xx_ring, o_ring = ring[6:9]
        n_stats = sb("n_stats", [P, 2, TILES, 6])
        n_mv = sb("n_mv", [P, 2, 2, TILES, 2])
        n_sd = sb("n_sd", [P, 3, TILES])
        n_rs = sb("n_rs", [P, 3, 2, TILES])
        n_c, n_y = buf[6:8], buf[8:10]
        n_nm = sb("n_nm", [P, TILES])
        n_shift = sb("n_shift", [P, 2, TILES])
        n_t = dict(zip("z12gq", (flat(b[:, :, :]) for b in buf[10:15])))
        n_h = [flat(b[:, :, :]) for b in buf[15:17]]
        N_A, N_G, N_5, N_3 = bank[4:8]

        n_loaded, n_stored = ring_sems("loaded"), ring_sems("stored")
        NODE_STAGES = dict(
            bn="k3", ag="k2", sd="x1e", rs="nB", ce="idx", no="nA", TX="TA", zT="zAT", m1="m1", x1T="x1T", m2="m2",
            x2T="x2T", m3="m3", xx="U", bn2="bn2", ag2="ag2", sd2="sd2", rs2="rs2", c2="c2", y2="x2e", Tg="Tx1",
            gT="feat", mr="mR", hT="z1T", sq="z1", ss="Tz1", sd3="sd3", nm="k1", rs3="rs3", m5="Tx2", v="R", fin="dv")
        S = {k: stage(v) for k, v in NODE_STAGES.items()}

        class Nodes(Part):

            def __init__(self, base, n, shift=0, dve_norm=False):
                Part.__init__(self, n, 8, shift)
                self.base, self.dve_norm = base, dve_norm

            def rows_of(self, turn, ap):
                if self.overlaps(turn):
                    a = ap[N - ROWS:N, :]
                else:
                    a = ap[bass.ds((turn.g + self.base) * ROWS, ROWS), :]
                return a.rearrange("(p j) d -> p (j d)", p=P)

            def overlaps(self, turn):
                return isinstance(turn.g, int) and turn.g + self.base == NG - 1

        def node_sp(sp, nodes):
            def loads_stores(t):
                if c := t.at(0):
                    if (count := due(S["xx"], t.through(0) - RING)) is not None:
                        sp.wait_ge(S["xx"], count)
                    sp.dma_start(flat(x_ring[:, c.s, :, :]), nodes.rows_of(c, x)).then_inc(n_loaded[c.s], 16)
                if c := t.at(8):
                    if (count := due(S["fin"], t.through(8))) is not None:
                        sp.wait_ge(S["fin"], count)
                    if nodes.overlaps(c):
                        p = (c.g - 1) % RING
                        if (count := due(n_stored[p], 16 * ((c.g - 1) // RING + 1))) is not None:
                            sp.wait_ge(n_stored[p], count)
                    sp.dma_start(nodes.rows_of(c, out), flat(o_ring[:, c.s, :, :])).then_inc(n_stored[c.s], 16)
            return [(nodes, loads_stores)]

        def node_stored(sp, n):
            for s in range(RING):
                if (count := due(n_stored[s], 16 * uses(n, s))) is not None:
                    sp.wait_ge(n_stored[s], count)

        def node_dve(dve, nodes):
            def stats(c, src_ring, k, bn):
                for j in range(TILES):
                    last = dve.bn_stats(n_stats[:, k, j, :], src_ring[:, c.s, j, :])
                last.then_inc(S[bn], 1)

            def moments(c, k, ag):
                for j in range(TILES):
                    last = dve.bn_aggr(n_mv[:, k, c.s % 2, j, :], n_stats[:, k, j, :])
                last.then_inc(S[ag], 1)

            def first(t):
                if c := t.at(8):
                    if (count := due(S["rs3"], t.through(8))) is not None:
                        dve.wait_ge(S["rs3"], count)
                    if (count := due(S["m5"], t.through(8))) is not None:
                        dve.wait_ge(S["m5"], count)
                    if (count := due(n_stored[c.s], 16 * c.r)) is not None:
                        dve.wait_ge(n_stored[c.s], count)
                    for j in range(TILES):
                        last = dve.scalar_tensor_tensor(out=o_ring[:, c.s, j, :], in0=N_5[:, j * P:(j + 1) * P],
                                                        scalar=n_rs[:, 2, c.s % 2, j:j + 1], in1=bias_bc["two"][:, :],
                                                        op0=ALU.mult, op1=ALU.add)
                    last.then_inc(S["v"], 1)
                    if (count := due(S["v"], t.through(8))) is not None:
                        dve.wait_ge(S["v"], count)
                    dve.scalar_tensor_tensor(out=flat(o_ring[:, c.s, :, :]), in0=flat(o_ring[:, c.s, :, :]), scalar=0.0,
                                             in1=flat(xx_ring[:, c.s, :, :]), op0=ALU.max,
                                             op1=ALU.add).then_inc(S["fin"], 1)
                if c := t.at(1):
                    if (count := due(n_loaded[c.s], 16 * (c.r + 1))) is not None:
                        dve.wait_ge(n_loaded[c.s], count)
                    if (count := due(S["ag"], t.before(1))) is not None:
                        dve.wait_ge(S["ag"], count)
                    stats(c, x_ring, 0, "bn")
                if c := t.at(5):
                    if (count := due(S["sd2"], t.through(5))) is not None:
                        dve.wait_ge(S["sd2"], count)
                    if (count := due(S["y2"], t.before(5) - 1)) is not None:
                        dve.wait_ge(S["y2"], count)
                    dve.reciprocal(n_rs[:, 1, c.s % 2, :], n_sd[:, 1, :]).then_inc(S["rs2"], 1)
                    if nodes.dve_norm:
                        if (count := due(S["rs2"], t.through(5))) is not None:
                            dve.wait_ge(S["rs2"], count)
                        dve.scalar_tensor_tensor(out=n_shift[:, c.s % 2, :], in0=n_mv[:, 1, c.s % 2, :, 0], scalar=-1.0,
                                                 in1=n_rs[:, 1, c.s % 2, :], op0=ALU.mult,
                                                 op1=ALU.mult).then_inc(S["c2"], 1)
                if c := t.at(2):
                    if (count := due(S["sd"], t.through(2))) is not None:
                        dve.wait_ge(S["sd"], count)
                    if (count := due(S["no"], t.before(2) - 1)) is not None:
                        dve.wait_ge(S["no"], count)
                    dve.reciprocal(n_rs[:, 0, c.s % 2, :], n_sd[:, 0, :]).then_inc(S["rs"], 1)
                if (count := due(S["bn"], t.through(1))) is not None:
                    dve.wait_ge(S["bn"], count)
                if (count := due(S["sd"], t.before(1) - 1)) is not None:
                    dve.wait_ge(S["sd"], count)
                if (count := due(S["ce"], t.before(1) - 1)) is not None:
                    dve.wait_ge(S["ce"], count)
                if c := t.at(7):
                    if (count := due(S["sd3"], t.through(7))) is not None:
                        dve.wait_ge(S["sd3"], count)
                    dve.tensor_scalar(n_nm[:, :], n_sd[:, 2, :], NORM_EPS, None, ALU.max).then_inc(S["nm"], 1)
                if c := t.at(1):
                    moments(c, 0, "ag")

            def second(t):
                if c := t.at(4):
                    if (count := due(S["m3"], t.through(4))) is not None:
                        dve.wait_ge(S["m3"], count)
                    if (count := due(S["fin"], t.through(4) - RING)) is not None:
                        dve.wait_ge(S["fin"], count)
                    dve.scalar_tensor_tensor(out=flat(xx_ring[:, c.s, :, :]), in0=N_3[:, :], scalar=0.0,
                                             in1=flat(x_ring[:, c.s, :, :]), op0=ALU.max,
                                             op1=ALU.add).then_inc(S["xx"], 1)
                    if (count := due(S["xx"], t.through(4))) is not None:
                        dve.wait_ge(S["xx"], count)
                    if (count := due(S["ag2"], t.before(4))) is not None:
                        dve.wait_ge(S["ag2"], count)
                    stats(c, xx_ring, 1, "bn2")
                if (count := due(S["bn2"], t.through(4))) is not None:
                    dve.wait_ge(S["bn2"], count)
                if (count := due(S["sd2"], t.before(4) - 1)) is not None:
                    dve.wait_ge(S["sd2"], count)
                if (count := due(S["c2"], t.before(4) - 1)) is not None:
                    dve.wait_ge(S["c2"], count)
                if c := t.at(7):
                    if (count := due(S["nm"], t.through(7))) is not None:
                        dve.wait_ge(S["nm"], count)
                    if (count := due(S["v"], t.before(8))) is not None:
                        dve.wait_ge(S["v"], count)
                    dve.reciprocal(n_rs[:, 2, c.s % 2, :], n_nm[:, :]).then_inc(S["rs3"], 1)
                if c := t.at(4):
                    moments(c, 1, "ag2")
                if nodes.dve_norm and (c := t.at(5)):
                    if (count := due(S["c2"], t.through(5))) is not None:
                        dve.wait_ge(S["c2"], count)
                    if (count := due(S["Tg"], t.before(5))) is not None:
                        dve.wait_ge(S["Tg"], count)
                    for j in range(TILES):
                        last = dve.tensor_scalar(n_y[1][:, j, :], xx_ring[:, c.s, j, :],
                                                 n_rs[:, 1, c.s % 2, j:j + 1], n_shift[:, c.s % 2, j:j + 1],
                                                 ALU.mult, ALU.add)
                    last.then_inc(S["y2"], 1)

            return [(nodes, first), (nodes, second)]

        def node_pool(pool, nodes):
            def norm(c, src_ring, k, ag, rs, ce, no, T, value, before):
                if (count := due(S[ag], value)) is not None:
                    pool.wait_ge(S[ag], count)
                if (count := due(S[no], before)) is not None:
                    pool.wait_ge(S[no], count)
                pool.tensor_tensor(n_c[k][:, :, :], src_ring[:, c.s, :, :], per_row(n_mv[:, k, c.s % 2, :, 0]),
                                   ALU.subtract).then_inc(S[ce], 1)
                if (count := due(S[rs], value)) is not None:
                    pool.wait_ge(S[rs], count)
                if (count := due(S[ce], value)) is not None:
                    pool.wait_ge(S[ce], count)
                if (count := due(S[T], before)) is not None:
                    pool.wait_ge(S[T], count)
                pool.tensor_tensor(n_y[k][:, :, :], n_c[k][:, :, :], per_row(n_rs[:, k, c.s % 2, :]),
                                   ALU.mult).then_inc(S[no], 1)

            def norms(t):
                if not nodes.dve_norm and (c := t.at(5)):
                    norm(c, xx_ring, 1, "ag2", "rs2", "c2", "y2", "Tg", t.through(5), t.before(5))
                if c := t.at(2):
                    norm(c, x_ring, 0, "ag", "rs", "ce", "no", "TX", t.through(2), t.before(2))
            return [(nodes, norms)]

        def node_act(act, nodes):
            def first(t):
                if c := t.at(4):
                    if (count := due(S["m2"], t.through(4))) is not None:
                        act.wait_ge(S["m2"], count)
                    if (count := due(S["m3"], t.before(4))) is not None:
                        act.wait_ge(S["m3"], count)
                    act.activation(n_t["2"], N_A[:, :], ACT.Relu, bias=bias_col[:, 1:2]).then_inc(S["x2T"], 1)
                if c := t.at(5):
                    if (count := due(S["ag2"], t.through(5))) is not None:
                        act.wait_ge(S["ag2"], count)
                    if (count := due(S["rs2"], t.before(5))) is not None:
                        act.wait_ge(S["rs2"], count)
                    act.activation(n_sd[:, 1, :], n_mv[:, 1, c.s % 2, :, 1], ACT.Sqrt,
                                   bias=eps_col[:, 0:1]).then_inc(S["sd2"], 1)
                if c := t.at(2):
                    if (count := due(S["ag"], t.through(2))) is not None:
                        act.wait_ge(S["ag"], count)
                    if (count := due(S["rs"], t.before(2))) is not None:
                        act.wait_ge(S["rs"], count)
                    act.activation(n_sd[:, 0, :], n_mv[:, 0, c.s % 2, :, 1], ACT.Sqrt,
                                   bias=eps_col[:, 0:1]).then_inc(S["sd"], 1)
                if c := t.at(7):
                    if (count := due(S["ss"], t.through(7))) is not None:
                        act.wait_ge(S["ss"], count)
                    if (count := due(S["nm"], t.before(7))) is not None:
                        act.wait_ge(S["nm"], count)
                    act.activation(n_sd[:, 2, :], N_G[:, 0:TILES], ACT.Sqrt).then_inc(S["sd3"], 1)
                if c := t.at(3):
                    if (count := due(S["TX"], t.through(3))) is not None:
                        act.wait_ge(S["TX"], count)
                    if (count := due(S["m1"], t.before(3))) is not None:
                        act.wait_ge(S["m1"], count)
                    act.activation(n_t["z"], N_A[:, :], ACT.Relu).then_inc(S["zT"], 1)

            def second(t):
                if c := t.at(6):
                    if (count := due(S["Tg"], t.through(6))) is not None:
                        act.wait_ge(S["Tg"], count)
                    if (count := due(S["mr"], t.before(6))) is not None:
                        act.wait_ge(S["mr"], count)
                    act.activation(n_t["g"], N_G[:, :], ACT.Relu).then_inc(S["gT"], 1)
                if c := t.at(3):
                    if (count := due(S["m1"], t.through(3))) is not None:
                        act.wait_ge(S["m1"], count)
                    if (count := due(S["m2"], t.before(3))) is not None:
                        act.wait_ge(S["m2"], count)
                    act.activation(n_t["1"], N_A[:, :], ACT.Relu, bias=bias_col[:, 0:1]).then_inc(S["x1T"], 1)

            def third(t):
                if c := t.at(6):
                    if (count := due(S["mr"], t.through(6))) is not None:
                        act.wait_ge(S["mr"], count)
                    if (count := due(S["ss"], t.through(7))) is not None:
                        act.wait_ge(S["ss"], count)
                    act.activation(n_t["q"], N_G[:, :], ACT.Square, bias=bias_col[:, 2:3]).then_inc(S["sq"], 1)
                    if (count := due(S["m5"], t.before(6) - 1)) is not None:
                        act.wait_ge(S["m5"], count)
                    act.activation(n_h[c.s % 2], N_G[:, :], ACT.Relu, bias=bias_col[:, 2:3]).then_inc(S["hT"], 1)
            return [(nodes, first), (nodes, second), (nodes, third)]

        def node_pe(pe, nodes):
            def sums(t):
                if c := t.at(7):
                    if (count := due(S["sq"], t.through(7))) is not None:
                        pe.wait_ge(S["sq"], count)
                    if (count := due(S["hT"], t.through(7))) is not None:
                        pe.wait_ge(S["hT"], count)
                    for j in range(TILES):
                        last = pe.matmul(N_G[:, j:j + 1], n_t["q"][:, j * P:(j + 1) * P], ones_col[:, :],
                                         start=True, stop=True)
                    last.then_inc(S["ss"], 1)

            def first(t):
                if c := t.at(3):
                    if (count := due(S["no"], t.through(3))) is not None:
                        pe.wait_ge(S["no"], count)
                    if (count := due(S["x2T"], t.before(3))) is not None:
                        pe.wait_ge(S["x2T"], count)
                    transposes(pe, N_A, n_y[0], S["TX"])
                if c := t.at(4):
                    if (count := due(S["x2T"], t.through(4))) is not None:
                        pe.wait_ge(S["x2T"], count)
                    if (count := due(S["xx"], t.before(4))) is not None:
                        pe.wait_ge(S["xx"], count)
                    rows_matmul(pe, N_3, n_t["2"], "gcn3", "gcn3", S["m3"])

            def second(t):
                if c := t.at(6):
                    if (count := due(S["y2"], t.through(6))) is not None:
                        pe.wait_ge(S["y2"], count)
                    if (count := due(S["sd3"], t.through(7))) is not None:
                        pe.wait_ge(S["sd3"], count)
                    transposes(pe, N_G, n_y[1], S["Tg"])
                if c := t.at(3):
                    if (count := due(S["zT"], t.through(3))) is not None:
                        pe.wait_ge(S["zT"], count)
                    pe.matmul(N_A[:, :], w_sb["gcn1"][:, :], n_t["z"], start=True, stop=True).then_inc(S["m1"], 1)

            def third(t):
                if c := t.at(6):
                    if (count := due(S["gT"], t.through(6))) is not None:
                        pe.wait_ge(S["gT"], count)
                    pe.matmul(N_G[:, :], w_sb["self1"][:, :], n_t["g"], start=True, stop=True).then_inc(S["mr"], 1)
                if c := t.at(3):
                    if (count := due(S["x1T"], t.through(3))) is not None:
                        pe.wait_ge(S["x1T"], count)
                    pe.matmul(N_A[:, :], w_sb["gcn2"][:, :], n_t["1"], start=True, stop=True).then_inc(S["m2"], 1)
                if c := t.at(7):
                    if (count := due(S["hT"], t.through(7))) is not None:
                        pe.wait_ge(S["hT"], count)
                    if (count := due(S["v"], t.through(8))) is not None:
                        pe.wait_ge(S["v"], count)
                    rows_matmul(pe, N_5, n_h[c.s % 2], "self2", None, S["m5"])

            return [(nodes, sums), (nodes, first), (nodes, second), (nodes, third)]
        EG = -(-E // ROWS)
        EP = EG * ROWS
        ET = EP // P
        CW = 2 * P
        CR = EP // CW
        CF, CT = E // CW, E % CW
        assert EP % CW == 0 and CT > 0 and CF == CR - 1

        def scratch(name, shape, dt=F32):
            return nc.dram_tensor(name, shape, dt, kind="Internal").ap()

        node_table = scratch("node_table", [N, 2])
        table = {k: scratch(f"table{k}", [2 * EP, P]) for k in (1, 2, 3, 4)}
        self_rows = [scratch(f"self_rows{k}", [EP, P]) for k in range(2)]
        x_dst = scratch("x_dst", [EP, P])
        xx_dst = scratch("xx_dst", [EP, P])
        segment_rows = scratch("segment_rows", [2, EP], BF16)
        carry_a = scratch("carry_a", [CR, 3])
        carry_b = scratch("carry_b", [2, CR])

        DINV, WEIGHT, CINV, CD, OWN = range(5)
        edge_f = sb("edge_f", [P, ET, 5])
        SRC, DST, SCAT, TAB = range(4)
        edge_i = sb("edge_i", [P, ET, 4], I32)
        bias_bc = {k: sb(f"bias_bc_{k}", [P, P]) for k in ("gcn1", "gcn2", "gcn3", "two")}
        bias_bc_in = sem("bias_bc_in")

        q_int = sb("q_int", [CR, 2, CW], I32)
        q_ends = sb("q_ends", [CR, 2], I32)
        q_d = sb("q_d", [CR, CW + 2])
        Q = {k: sb(f"q_{k}", [CR, CW]) for k in
             ("same last ones cnt ws pm cntF wsF deg sd y y2 y3 wmax").split()}
        q_out = sb("q_out", [CR, 7, CW])
        q_seg = sb("q_seg", [CR, 2, CW], BF16)
        q_carry = sb("q_carry", [CR, 3])
        q_row = sb("q_row", [1, 3, CR])
        q_full = sb("q_full", [1, 2, CR])
        q_in = sb("q_in", [CR, 2])
        own_i = sb("own_i", [P, ET], I32)
        q_zero = buf[0]
        p_set, p_load, p_dve, p_act, p_seg, p_c1, p_c2, p_c3, p_c4, p_T, p_own, p_q, p_deg, p_table0 = (
            sem(f"p_{k}") for k in "set load dve act seg c1 c2 c3 c4 T own q deg table0".split())
        N_SET = 9
        FILL = N // P * 2

        def prep_pool(pool):
            pool.memset(q_int[:, 0, :], 0).then_inc(p_set, 1)
            pool.memset(q_int[:, 1, :], N).then_inc(p_set, 1)
            pool.memset(q_ends[:, 0:1], -1).then_inc(p_set, 1)
            pool.memset(q_ends[:, 1:2], N + 1).then_inc(p_set, 1)
            pool.memset(q_out[:, 3, :], 0.0).then_inc(p_set, 1)
            pool.memset(Q["ones"][:, :], 1.0).then_inc(p_set, 1)
            pool.memset(q_in[:, :], 0.0).then_inc(p_set, 1)
            pool.memset(flat(q_zero[:, :, :]), 0.0).then_inc(p_set, 1)
            pool.memset(edge_i[:, :, TAB], 0).then_inc(p_set, 1)
            pool.iota(own_i[:, :], pattern=[[P, ET]], base=EP, channel_multiplier=1).then_inc(p_own, 1)

        def prep_loads(sp):
            sp.wait_ge(p_set, N_SET)
            grid = [a[0:CF * CW].rearrange("(r c) -> r c", c=CW) for a in (src, dst, edge_weight)]
            rest = [a[CF * CW:E].rearrange("(a c) -> a c", a=1) for a in (src, dst, edge_weight)]
            for k in range(3):
                to = q_int[:, k, :] if k < 2 else q_out[:, 3, :]
                sp.dma_start(to[0:CF, :], grid[k]).then_inc(p_load, 16)
                sp.dma_start(to[CF:CR, 0:CT], rest[k]).then_inc(p_load, 16)
            sp.dma_start(q_ends[1:CR, 0:1], grid[1][:, CW - 1:CW], allow_slow_non_contiguous=True).then_inc(p_load, 16)
            sp.dma_start(q_ends[0:CF - 1, 1:2], grid[1][1:CF, 0:1], allow_slow_non_contiguous=True).then_inc(p_load, 16)
            sp.dma_start(q_ends[CF - 1:CF, 1:2], rest[1][:, 0:1], allow_slow_non_contiguous=True).then_inc(p_load, 16)
            flat_table = node_table.rearrange("n k -> (n k)")
            part = flat_table[0:P * FILL].rearrange("(p c) -> p c", c=FILL)
            zero = flat(q_zero[:, :, :])
            n = 0
            for c in range(0, FILL, ROWS):
                w = min(ROWS, FILL - c)
                sp.dma_start(part[:, c:c + w], zero[:, 0:w]).then_inc(p_table0, 16)
                n += 1
            tail = N * 2 - P * FILL
            if tail:
                sp.dma_start(flat_table[P * FILL:N * 2].rearrange("(a c) -> a c", a=1), zero[0:1, 0:tail])\
                  .then_inc(p_table0, 16)
                n += 1
            return n

        def prep_carries(sp, zero_dmas):
            sp.wait_ge(p_seg, 1)
            for k in range(2):
                sp.dma_start(segment_rows[k, :].rearrange("(r c) -> r c", c=CW), q_seg[:, k, :]).then_inc(p_c4, 16)
            sp.wait_ge(p_c1, 1)
            sp.dma_start(carry_a, q_carry[:, :]).then_inc(p_c2, 16)
            sp.wait_ge(p_c2, 16)
            sp.dma_start(q_row[:, :, :], carry_a.rearrange("(a r) k -> a k r", a=1),
                         allow_slow_non_contiguous=True).then_inc(p_c2, 16)
            sp.wait_ge(p_c1, 2)
            sp.dma_start(carry_b.rearrange("(a k) r -> a k r", a=1), q_full[:, :, :]).then_inc(p_c3, 16)
            sp.wait_ge(p_c3, 16)
            sp.dma_start(q_in[1:CR, :], carry_b[:, 0:CR - 1].rearrange("k r -> r k"),
                         allow_slow_non_contiguous=True).then_inc(p_c3, 16)
            sp.wait_ge(p_c3, 32)
            sp.wait_ge(p_c4, 32)
            sp.wait_ge(p_table0, 16 * zero_dmas)

        def prep_dve(dve):
            count = [0]

            def chain(ins):
                count[0] += 1
                ins.then_inc(p_dve, 1)
                dve.wait_ge(p_dve, count[0])

            dve.wait_ge(p_load, 16 * 9)
            dve.wait_ge(p_set, N_SET)
            dve.tensor_copy(q_d[:, 0:1], q_ends[:, 0:1])
            dve.tensor_copy(q_d[:, CW + 1:CW + 2], q_ends[:, 1:2])
            chain(dve.tensor_copy(q_d[:, 1:CW + 1], q_int[:, 1, :]))
            d = q_d[:, 1:CW + 1]
            dve.tensor_tensor(Q["last"][:, :], d, q_d[:, 2:CW + 2], ALU.not_equal)
            chain(dve.tensor_tensor(Q["same"][:, :], d, q_d[:, 0:CW], ALU.is_equal))
            dve.tensor_copy(q_seg[:, 0, :], Q["same"][:, :])
            dve.tensor_scalar(q_seg[:, 1, :], Q["same"][:, :], -1.0, FAR, ALU.add, ALU.mult).then_inc(p_seg, 1)
            w = q_out[:, 3, :]
            dve.tensor_tensor_scan(Q["cnt"][:, :], Q["same"][:, :], Q["ones"][:, :], 0.0, ALU.mult, ALU.add)
            dve.tensor_tensor_scan(Q["ws"][:, :], Q["same"][:, :], w, 0.0, ALU.mult, ALU.add)
            chain(dve.tensor_tensor_scan(Q["pm"][:, :], Q["same"][:, :], Q["ones"][:, :], 1.0, ALU.mult, ALU.mult))
            for k, name in enumerate(("cnt", "ws", "pm")):
                last = dve.tensor_copy(q_carry[:, k:k + 1], Q[name][:, CW - 1:CW])
            last.then_inc(p_c1, 1)
            dve.tensor_copy(q_out[:, 0, :], q_int[:, 0, :])
            dve.tensor_scalar(q_out[:, 1, :], d, float(N - 1), None, ALU.min)
            chain(dve.scalar_tensor_tensor(out=Q["y3"][:, :], in0=Q["last"][:, :], scalar=-2.0 * N, in1=d,
                                           op0=ALU.mult, op1=ALU.add))
            chain(dve.tensor_scalar(q_out[:, 2, :], Q["y3"][:, :], 2.0 * N, None, ALU.add))
            dve.wait_ge(p_c2, 32)
            for k in range(2):
                last = dve.tensor_tensor_scan(q_full[:, k, :], q_row[:, 2, :], q_row[:, k, :], 0.0, ALU.mult, ALU.add)
            last.then_inc(p_c1, 1)
            dve.wait_ge(p_c3, 32)
            for k, (a, b) in enumerate((("cnt", "cntF"), ("ws", "wsF"))):
                op = dve.scalar_tensor_tensor(out=Q[b][:, :], in0=Q["pm"][:, :], scalar=q_in[:, k:k + 1],
                                              in1=Q[a][:, :], op0=ALU.mult, op1=ALU.add)
            chain(op)
            dve.tensor_scalar(Q["wmax"][:, :], Q["wsF"][:, :], NORM_EPS, None, ALU.max)
            dve.tensor_scalar(Q["deg"][:, :], Q["cntF"][:, :], 1.0, None, ALU.add).then_inc(p_deg, 1)
            dve.wait_ge(p_act, 1)
            dve.reciprocal(q_out[:, 5, :], Q["wmax"][:, :])
            dve.reciprocal(Q["y3"][:, :], Q["cntF"][:, :])
            chain(dve.reciprocal(Q["y"][:, :], Q["sd"][:, :]))
            dve.tensor_tensor(q_out[:, 6, :], q_out[:, 5, :], Q["y3"][:, :], ALU.mult)
            chain(dve.tensor_tensor(Q["y2"][:, :], Q["y"][:, :], Q["y"][:, :], ALU.mult))
            chain(dve.tensor_tensor(Q["y3"][:, :], Q["y2"][:, :], Q["deg"][:, :], ALU.mult))
            chain(dve.tensor_scalar(Q["y2"][:, :], Q["y3"][:, :], -0.5, 1.5, ALU.mult, ALU.add))
            dve.tensor_tensor(q_out[:, 4, :], Q["y"][:, :], Q["y2"][:, :], ALU.mult).then_inc(p_q, 1)
            dve.wait_ge(p_T, 14)
            dve.wait_ge(p_own, 1)
            for a in range(7):
                for k in range(2):
                    n = 2 * a + k
                    col = bank[n // 5][:, (n % 5) * CR:(n % 5) * CR + CR]
                    to = edge_i[:, k::2, a] if a < 3 else edge_f[:, k::2, {3: WEIGHT, 4: DINV, 5: CINV, 6: CD}[a]]
                    dve.tensor_copy(to, col)
            dve.tensor_copy(edge_f[:, :, OWN], own_i[:, :])

        def prep_act(act):
            act.wait_ge(p_deg, 1)
            act.activation(Q["sd"][:, :], Q["deg"][:, :], ACT.Sqrt).then_inc(p_act, 1)

        def prep_pe(pe):
            pe.wait_ge(ident_done, 1)
            pe.wait_ge(p_q, 1)
            for a in range(7):
                for k in range(2):
                    n = 2 * a + k
                    pe.transpose(bank[n // 5][:, (n % 5) * CR:(n % 5) * CR + CR],
                                 q_out[:, a, k * P:(k + 1) * P], ident[0:CR, 0:CR]).then_inc(p_T, 1)

        st_i = sb("st_i", [P, RING, TILES, 4], I32)
        st_f = sb("st_f", [P, RING, TILES, 5])
        t_val = sb("t_val", [P, RING, TILES, 2])
        t_staged = stage("staged")
        t_scattered = ring_sems("scattered")

        def group_of(per_edge, c):
            return per_edge[:, bass.ds(c.g * TILES, TILES), :]

        def table_dve(dve):
            def step(t):
                if c := t.at(0):
                    if (count := due(t_scattered[c.s], 16 * TILES * c.r)) is not None:
                        dve.wait_ge(t_scattered[c.s], count)
                    dve.tensor_copy(st_i[:, c.s, :, :], group_of(edge_i, c))
                    dve.tensor_scalar(t_val[:, c.s, :, 0], edge_f[:, bass.ds(c.g * TILES, TILES), OWN],
                                      -float(EP), None, ALU.add)
                    dve.tensor_copy(t_val[:, c.s, :, 1], edge_f[:, bass.ds(c.g * TILES, TILES), DINV])\
                       .then_inc(t_staged, 1)
            return step

        def table_pool(pool):
            limit = Limit(pool, node_table)

            def step(t):
                if c := t.at(1):
                    if (count := due(t_staged, t.through(1))) is not None:
                        pool.wait_ge(t_staged, count)
                    limit.set()
                    for j in range(TILES):
                        pool.indirect_dma_start(
                            out=node_table, out_offset=bass.IndirectOffsetOnAxis(ap=st_i[:, c.s, j, SCAT:SCAT + 1], axis=0),
                            in_=t_val[:, c.s, j, :], in_offset=None, bounds_check=limit.register,
                            oob_is_err=False).then_inc(t_scattered[c.s], 16)
            return step

        def table_scattered(pool):
            for s in range(RING):
                if (count := due(t_scattered[s], 16 * TILES * uses(EG, s))) is not None:
                    pool.wait_ge(t_scattered[s], count)

        xs_ring, xd_ring, t1b_ring, t2b_ring, t3b_ring, t4b_ring, z1_ring, r_ring = ring[0:8]
        (f_zA, f_zB, _, f_zBT, f_S, f_U, f_v, f_x1T, f_x2T, f_y2) = buf[0:10]
        (f_xx, f_c2, f_gT, f_z1T, f_c) = buf[10:15]
        f_pg = sb("f_pg", [P, RING, TILES, 2])
        f_small = sb("f_small", [P, 24, TILES])
        f_stats = sb("f_stats", [P, 3, TILES, 6])
        f_mv = sb("f_mv", [P, 3, TILES, 2])
        f_SS = (f_S, f_c)
        seg_ring = sb("seg_ring", [P, RING, ROWS], BF16)
        f_seg_in = ring_sems("seg_in")
        FIRST_LAG = 6
        F = {k: stage(k) for k in (
            "staged numbers idx bn ag sd s1 dv s_b tb nA nB TA TB zBT scan U mU v z1 Tz1 z1T mR R m1 x1T m2 x2T "
            "Tx1 x1e Tx2 x2e m3 xx bn2 ag2 sd2 rs2 c2 y2 Tg gT mf feat mr sq sd3 nm rs3 h k1 k2 k3").split()}
        f_pg_in, f_xs_in, f_xd_in = ring_sems("pg_in"), ring_sems("xs_in"), ring_sems("xd_in")
        f_xd_out, f_z1_out, f_r_out = ring_sems("xd_out"), ring_sems("z1_out"), ring_sems("r_out")
        f_t_out = {k: ring_sems(f"t{k}_out") for k in (1, 2, 3, 4)}

        def cols(b):
            return b[:, :, :].rearrange("p j d -> p (j d)")

        def tiles(b):
            return b.rearrange("p (j d) -> p j d", j=TILES)

        def edge_rows(table_ap, c, base=0):
            return table_ap[bass.ds(c.g * ROWS + base, ROWS), :].rearrange("(j p) d -> p j d", p=P)

        class Limit:

            made = 0

            def __init__(self, pool, array):
                below, self.register = (pool.alloc_register(f"limit_{Limit.made}_{i}") for i in range(2))
                Limit.made += 1
                pool.reg_mov(below, array.shape[0] - 2)
                self.set = lambda: pool.reg_add(self.register, below, 1)

        def gathers(pool, c, to, from_, limit, k, done):
            limit.set()
            for j in range(TILES):
                pool.indirect_dma_start(
                    out=to[:, c.s, j, :], out_offset=None, in_=from_,
                    in_offset=bass.IndirectOffsetOnAxis(ap=st_i[:, c.s, j, k:k + 1], axis=0),
                    bounds_check=limit.register, oob_is_err=False).then_inc(done[c.s], 16)

        ALL = 16 * TILES

        def first_pool(pool):
            limit = Limit(pool, x)

            def step(t):
                if c := t.at(1):
                    if (count := due(F["staged"], t.through(1))) is not None:
                        pool.wait_ge(F["staged"], count)
                    if (count := due(F["dv"], t.through(1) - RING)) is not None:
                        pool.wait_ge(F["dv"], count)
                    if (count := due(F["idx"], t.through(1) - RING)) is not None:
                        pool.wait_ge(F["idx"], count)
                    gathers(pool, c, f_pg, node_table, limit, SRC, f_pg_in)
                    if (count := due(F["nA"], t.through(1) - RING)) is not None:
                        pool.wait_ge(F["nA"], count)
                    if (count := due(f_xd_out[c.s], 16 * c.r)) is not None:
                        pool.wait_ge(f_xd_out[c.s], count)
                    gathers(pool, c, xd_ring, x, limit, DST, f_xd_in)
                    if (count := due(F["xx"], t.through(1) - RING)) is not None:
                        pool.wait_ge(F["xx"], count)
                    gathers(pool, c, xs_ring, x, limit, SRC, f_xs_in)
            pipeline(pool, EG, FIRST_LAG, step)

        def load_segments(sp, c, k, done):
            sp.dma_start(seg_ring[:, c.s, :], segment_rows[k:k + 1, bass.ds(c.g * ROWS, ROWS)].broadcast_to([P, ROWS]))\
              .then_inc(done[c.s], 16)

        def first_sp(sp):
            def step(t):
                if c := t.at(1):
                    if (count := due(F["scan"], t.through(1) - RING)) is not None:
                        sp.wait_ge(F["scan"], count)
                    load_segments(sp, c, 0, f_seg_in)
                if c := t.at(2):
                    if (count := due(f_xd_in[c.s], ALL * (c.r + 1))) is not None:
                        sp.wait_ge(f_xd_in[c.s], count)
                    sp.dma_start(edge_rows(x_dst, c), xd_ring[:, c.s, :, :]).then_inc(f_xd_out[c.s], 16)
                if c := t.at(4):
                    if (count := due(F["x1e"], t.through(4))) is not None:
                        sp.wait_ge(F["x1e"], count)
                    sp.dma_start(edge_rows(table[1], c, EP), t1b_ring[:, c.s, :, :]).then_inc(f_t_out[1][c.s], 16)
                    if (count := due(F["z1"], t.through(4))) is not None:
                        sp.wait_ge(F["z1"], count)
                    sp.dma_start(edge_rows(table[1], c), z1_ring[:, c.s, :, :]).then_inc(f_z1_out[c.s], 16)
                if c := t.at(5):
                    if (count := due(F["x2e"], t.through(5))) is not None:
                        sp.wait_ge(F["x2e"], count)
                    sp.dma_start(edge_rows(table[2], c, EP), t2b_ring[:, c.s, :, :]).then_inc(f_t_out[2][c.s], 16)
                    if (count := due(F["R"], t.through(5))) is not None:
                        sp.wait_ge(F["R"], count)
                    sp.dma_start(edge_rows(self_rows[0], c), r_ring[:, c.s, :, :]).then_inc(f_r_out[c.s], 16)
                if c := t.at(6):
                    if (count := due(F["feat"], t.through(6))) is not None:
                        sp.wait_ge(F["feat"], count)
                    sp.dma_start(edge_rows(table[3], c, EP), t3b_ring[:, c.s, :, :]).then_inc(f_t_out[3][c.s], 16)
                    if (count := due(F["h"], t.through(6))) is not None:
                        sp.wait_ge(F["h"], count)
                    sp.dma_start(edge_rows(table[4], c, EP), t4b_ring[:, c.s, :, :]).then_inc(f_t_out[4][c.s], 16)
            pipeline(sp, EG, FIRST_LAG, step)
            for s in range(RING):
                for group in (f_xd_out, f_z1_out, f_r_out, *f_t_out.values()):
                    if (count := due(group[s], 16 * uses(EG, s))) is not None:
                        sp.wait_ge(group[s], count)

        EQ, DV, T1, T2, SD, RS, SA, SB, TAm, TBm, SD2, RS2, SS, SD3, NM, RS3 = 0, 1, 2, 3, 4, 6, *range(8, 18)

        def first_dve(dve):
            def small(i, n=1):
                return f_small[:, i, :] if n == 1 else f_small[:, i:i + n, :]

            def step(t):
                if c := t.at(0):
                    for own in (f_pg_in, f_xs_in, f_xd_in):
                        if (count := due(own[c.s], ALL * c.r)) is not None:
                            dve.wait_ge(own[c.s], count)
                    dve.tensor_copy(st_i[:, c.s, :, :], group_of(edge_i, c)).then_inc(F["staged"], 1)
                if c := t.at(5):
                    if (count := due(F["sd2"], t.through(5))) is not None:
                        dve.wait_ge(F["sd2"], count)
                    if (count := due(F["y2"], t.before(5))) is not None:
                        dve.wait_ge(F["y2"], count)
                    dve.reciprocal(small(RS2), small(SD2)).then_inc(F["rs2"], 1)
                    if (count := due(F["rs2"], t.through(5))) is not None:
                        dve.wait_ge(F["rs2"], count)
                    if (count := due(F["c2"], t.before(5))) is not None:
                        dve.wait_ge(F["c2"], count)
                    dve.tensor_tensor(f_c2[:, :, :], f_xx[:, :, :], per_row(f_mv[:, 2, :, 0]),
                                      ALU.subtract).then_inc(F["c2"], 1)
                    if (count := due(F["c2"], t.through(5))) is not None:
                        dve.wait_ge(F["c2"], count)
                    if (count := due(F["Tg"], t.before(5))) is not None:
                        dve.wait_ge(F["Tg"], count)
                    dve.tensor_tensor(f_y2[:, :, :], f_c2[:, :, :], per_row(small(RS2)), ALU.mult).then_inc(F["y2"], 1)
                if c := t.at(3):
                    if (count := due(F["zBT"], t.through(3))) is not None:
                        dve.wait_ge(F["zBT"], count)
                    if (count := due(f_seg_in[c.s], 16 * (c.r + 1))) is not None:
                        dve.wait_ge(f_seg_in[c.s], count)
                    if (count := due(F["scan"], t.before(3))) is not None:
                        dve.wait_ge(F["scan"], count)
                    start = 0.0 if isinstance(c.g, int) and c.g == 0 else cols(f_SS[(c.s + 1) % 2])[:, ROWS - 1:ROWS]
                    dve.tensor_tensor_scan(cols(f_SS[c.s % 2]), seg_ring[:, c.s, :], cols(f_zBT), start,
                                           ALU.mult, ALU.add).then_inc(F["scan"], 1)
                    if (count := due(F["scan"], t.through(3))) is not None:
                        dve.wait_ge(F["scan"], count)
                    if (count := due(F["TA"], t.through(3))) is not None:
                        dve.wait_ge(F["TA"], count)
                    if (count := due(F["mU"], t.before(3))) is not None:
                        dve.wait_ge(F["mU"], count)
                    dve.tensor_tensor(cols(f_U), cols(f_SS[c.s % 2]), bank[5][:, :], ALU.add).then_inc(F["U"], 1)
                if c := t.at(6):
                    if (count := due(F["sd3"], t.through(6))) is not None:
                        dve.wait_ge(F["sd3"], count)
                    dve.tensor_scalar(small(NM), small(SD3), NORM_EPS, None, ALU.max).then_inc(F["nm"], 1)
                    if (count := due(F["nm"], t.through(6))) is not None:
                        dve.wait_ge(F["nm"], count)
                    if (count := due(F["h"], t.before(6))) is not None:
                        dve.wait_ge(F["h"], count)
                    dve.reciprocal(small(RS3), small(NM)).then_inc(F["rs3"], 1)
                if c := t.at(2):
                    if (count := due(f_xd_in[c.s], ALL * (c.r + 1))) is not None:
                        dve.wait_ge(f_xd_in[c.s], count)
                    if (count := due(f_xs_in[c.s], ALL * (c.r + 1))) is not None:
                        dve.wait_ge(f_xs_in[c.s], count)
                    if (count := due(F["ag"], t.before(2))) is not None:
                        dve.wait_ge(F["ag"], count)
                    for k, r in enumerate((xd_ring, xs_ring)):
                        for j in range(TILES):
                            last = dve.bn_stats(f_stats[:, k, j, :], r[:, c.s, j, :])
                    last.then_inc(F["bn"], 1)
                    if (count := due(F["bn"], t.through(2))) is not None:
                        dve.wait_ge(F["bn"], count)
                    if (count := due(F["nB"], t.before(2))) is not None:
                        dve.wait_ge(F["nB"], count)
                    if (count := due(F["tb"], t.before(2))) is not None:
                        dve.wait_ge(F["tb"], count)
                    if (count := due(f_pg_in[c.s], ALL * (c.r + 1))) is not None:
                        dve.wait_ge(f_pg_in[c.s], count)
                    dve.tensor_scalar(small(EQ), f_pg[:, c.s, :, 1], 0.0, None, ALU.is_equal).then_inc(F["k1"], 1)
                    for k in range(2):
                        for j in range(TILES):
                            last = dve.bn_aggr(f_mv[:, k, j, :], f_stats[:, k, j, :])
                    last.then_inc(F["ag"], 1)
                    if (count := due(F["k1"], t.through(2))) is not None:
                        dve.wait_ge(F["k1"], count)
                    if (count := due(F["numbers"], t.through(2))) is not None:
                        dve.wait_ge(F["numbers"], count)
                    dve.tensor_tensor(small(DV), small(EQ), f_pg[:, c.s, :, 1], ALU.add).then_inc(F["dv"], 1)
                    dve.tensor_tensor(small(T1), small(EQ), st_f[:, c.s, :, OWN], ALU.mult).then_inc(F["k2"], 1)
                    if (count := due(F["k2"], t.through(2))) is not None:
                        dve.wait_ge(F["k2"], count)
                    dve.tensor_tensor(small(T2), small(T1), f_pg[:, c.s, :, 0], ALU.add).then_inc(F["k3"], 1)
                    if (count := due(F["sd"], t.through(2))) is not None:
                        dve.wait_ge(F["sd"], count)
                    dve.reciprocal(small(RS, 2), small(SD, 2)).then_inc(F["s1"], 1)
                    if (count := due(F["k3"], t.through(2))) is not None:
                        dve.wait_ge(F["k3"], count)
                    dve.tensor_copy(edge_i[:, bass.ds(c.g * TILES, TILES), TAB], small(T2)).then_inc(F["idx"], 1)
                    if (count := due(F["s1"], t.through(2))) is not None:
                        dve.wait_ge(F["s1"], count)
                    if (count := due(F["nA"], t.before(2))) is not None:
                        dve.wait_ge(F["nA"], count)
                    dve.tensor_tensor(small(SA), small(RS), st_f[:, c.s, :, DINV], ALU.mult)
                    dve.tensor_tensor(small(SB), small(RS + 1), small(DV), ALU.mult).then_inc(F["s_b"], 1)
                    if (count := due(F["s_b"], t.through(2))) is not None:
                        dve.wait_ge(F["s_b"], count)
                    dve.scalar_tensor_tensor(out=small(TAm), in0=f_mv[:, 0, :, 0], scalar=-1.0, in1=small(SA),
                                             op0=ALU.mult, op1=ALU.mult)
                    dve.scalar_tensor_tensor(out=small(TBm), in0=f_mv[:, 1, :, 0], scalar=-1.0, in1=small(SB),
                                             op0=ALU.mult, op1=ALU.mult).then_inc(F["tb"], 1)
                if c := t.at(3):
                    if (count := due(F["mU"], t.through(3))) is not None:
                        dve.wait_ge(F["mU"], count)
                    if (count := due(F["z1"], t.before(3))) is not None:
                        dve.wait_ge(F["z1"], count)
                    for j in range(TILES):
                        last = dve.scalar_tensor_tensor(out=f_v[:, j, :], in0=bank[5][:, j * P:(j + 1) * P],
                                                        scalar=st_f[:, c.s, j, DINV:DINV + 1], in1=bias_bc["gcn1"][:, :],
                                                        op0=ALU.mult, op1=ALU.add)
                    last.then_inc(F["v"], 1)
                if c := t.at(4):
                    if (count := due(F["m3"], t.through(4))) is not None:
                        dve.wait_ge(F["m3"], count)
                    if (count := due(F["c2"], t.through(5))) is not None:
                        dve.wait_ge(F["c2"], count)
                    if (count := due(F["bn2"], t.before(4))) is not None:
                        dve.wait_ge(F["bn2"], count)
                    dve.scalar_tensor_tensor(out=cols(f_xx), in0=bank[1][:, :], scalar=0.0,
                                             in1=flat(xs_ring[:, c.s, :, :]), op0=ALU.max, op1=ALU.add).then_inc(F["xx"], 1)
                    if (count := due(F["xx"], t.through(4))) is not None:
                        dve.wait_ge(F["xx"], count)
                    if (count := due(F["ag2"], t.before(4))) is not None:
                        dve.wait_ge(F["ag2"], count)
                    for j in range(TILES):
                        last = dve.bn_stats(f_stats[:, 2, j, :], f_xx[:, j, :])
                    last.then_inc(F["bn2"], 1)
                    if (count := due(F["mR"], t.through(4))) is not None:
                        dve.wait_ge(F["mR"], count)
                    if (count := due(f_r_out[c.s], 16 * c.r)) is not None:
                        dve.wait_ge(f_r_out[c.s], count)
                    if (count := due(F["bn2"], t.through(4))) is not None:
                        dve.wait_ge(F["bn2"], count)
                    for j in range(TILES):
                        last = dve.scalar_tensor_tensor(out=r_ring[:, c.s, j, :], in0=bank[6][:, j * P:(j + 1) * P],
                                                        scalar=st_f[:, c.s, j, DINV:DINV + 1], in1=bias_bc["gcn2"][:, :],
                                                        op0=ALU.mult, op1=ALU.add)
                    last.then_inc(F["R"], 1)
                    for j in range(TILES):
                        last = dve.bn_aggr(f_mv[:, 2, j, :], f_stats[:, 2, j, :])
                    last.then_inc(F["ag2"], 1)
                if c := t.at(0):
                    if (count := due(F["z1"], t.through(0) - RING)) is not None:
                        dve.wait_ge(F["z1"], count)
                    if (count := due(F["R"], t.through(0) - RING)) is not None:
                        dve.wait_ge(F["R"], count)
                    dve.tensor_copy(st_f[:, c.s, :, :], group_of(edge_f, c)).then_inc(F["numbers"], 1)
            pipeline(dve, EG, FIRST_LAG, step)

        def first_act(act):
            def small(i, n=1):
                return f_small[:, i, :] if n == 1 else f_small[:, i:i + n, :]

            def step(t):
                if c := t.at(4):
                    if (count := due(F["m2"], t.through(4))) is not None:
                        act.wait_ge(F["m2"], count)
                    if (count := due(F["m3"], t.before(4))) is not None:
                        act.wait_ge(F["m3"], count)
                    act.activation(cols(f_x2T), bank[3][:, :], ACT.Relu, bias=bias_col[:, 1:2]).then_inc(F["x2T"], 1)
                if c := t.at(3):
                    if (count := due(F["m1"], t.through(3))) is not None:
                        act.wait_ge(F["m1"], count)
                    if (count := due(F["m2"], t.before(3))) is not None:
                        act.wait_ge(F["m2"], count)
                    act.activation(cols(f_x1T), bank[0][:, :], ACT.Relu, bias=bias_col[:, 0:1]).then_inc(F["x1T"], 1)
                if c := t.at(4):
                    if (count := due(F["Tz1"], t.through(4))) is not None:
                        act.wait_ge(F["Tz1"], count)
                    if (count := due(F["mR"], t.before(4))) is not None:
                        act.wait_ge(F["mR"], count)
                    act.activation(cols(f_z1T), bank[1][:, :], ACT.Copy).then_inc(F["z1T"], 1)
                if c := t.at(6):
                    if (count := due(F["rs3"], t.through(6))) is not None:
                        act.wait_ge(F["rs3"], count)
                    if (count := due(f_t_out[4][c.s], 16 * c.r)) is not None:
                        act.wait_ge(f_t_out[4][c.s], count)
                    for j in range(TILES):
                        last = act.activation(t4b_ring[:, c.s, j, :], bank[7][:, j * P:(j + 1) * P], ACT.Relu,
                                              scale=small(RS3)[:, j:j + 1])
                    last.then_inc(F["h"], 1)
                if c := t.at(5):
                    if (count := due(F["Tg"], t.through(5))) is not None:
                        act.wait_ge(F["Tg"], count)
                    if (count := due(F["mr"], t.before(5))) is not None:
                        act.wait_ge(F["mr"], count)
                    act.activation(cols(f_gT), bank[4][:, :], ACT.Relu).then_inc(F["gT"], 1)
                if c := t.at(4):
                    if (count := due(F["Tx2"], t.through(4))) is not None:
                        act.wait_ge(F["Tx2"], count)
                    if (count := due(f_t_out[2][c.s], 16 * c.r)) is not None:
                        act.wait_ge(f_t_out[2][c.s], count)
                    act.activation(flat(t2b_ring[:, c.s, :, :]), bank[0][:, :], ACT.Copy).then_inc(F["x2e"], 1)
                if c := t.at(3):
                    if (count := due(F["Tx1"], t.through(3))) is not None:
                        act.wait_ge(F["Tx1"], count)
                    if (count := due(f_t_out[1][c.s], 16 * c.r)) is not None:
                        act.wait_ge(f_t_out[1][c.s], count)
                    act.activation(flat(t1b_ring[:, c.s, :, :]), bank[2][:, :], ACT.Copy).then_inc(F["x1e"], 1)
                if c := t.at(2):
                    if (count := due(F["ag"], t.through(2))) is not None:
                        act.wait_ge(F["ag"], count)
                    if (count := due(F["s1"], t.before(2))) is not None:
                        act.wait_ge(F["s1"], count)
                    act.activation(small(SD, 2), f_mv[:, 0:2, :, 1], ACT.Sqrt, bias=eps_col[:, 0:1]).then_inc(F["sd"], 1)
                if c := t.at(2):
                    if (count := due(F["tb"], t.through(2))) is not None:
                        act.wait_ge(F["tb"], count)
                    if (count := due(F["TA"], t.before(2))) is not None:
                        act.wait_ge(F["TA"], count)
                    for j in range(TILES):
                        last = act.activation(f_zA[:, j, :], xd_ring[:, c.s, j, :], ACT.Relu,
                                              scale=small(SA)[:, j:j + 1], bias=small(TAm)[:, j:j + 1])
                    last.then_inc(F["nA"], 1)
                if c := t.at(5):
                    if (count := due(F["mf"], t.through(5))) is not None:
                        act.wait_ge(F["mf"], count)
                    if (count := due(f_t_out[3][c.s], 16 * c.r)) is not None:
                        act.wait_ge(f_t_out[3][c.s], count)
                    act.activation(flat(t3b_ring[:, c.s, :, :]), bank[4][:, :], ACT.Relu).then_inc(F["feat"], 1)
                if c := t.at(2):
                    if (count := due(F["TB"], t.before(2))) is not None:
                        act.wait_ge(F["TB"], count)
                    for j in range(TILES):
                        last = act.activation(f_zB[:, j, :], xs_ring[:, c.s, j, :], ACT.Relu,
                                              scale=small(SB)[:, j:j + 1], bias=small(TBm)[:, j:j + 1])
                    last.then_inc(F["nB"], 1)
                if c := t.at(3):
                    if (count := due(F["v"], t.through(3))) is not None:
                        act.wait_ge(F["v"], count)
                    if (count := due(f_z1_out[c.s], 16 * c.r)) is not None:
                        act.wait_ge(f_z1_out[c.s], count)
                    if (count := due(F["Tz1"], t.through(3) - RING)) is not None:
                        act.wait_ge(F["Tz1"], count)
                    for j in range(TILES):
                        last = act.activation(z1_ring[:, c.s, j, :], f_v[:, j, :], ACT.Relu,
                                              scale=st_f[:, c.s, j, DINV:DINV + 1])
                    last.then_inc(F["z1"], 1)
                if c := t.at(4):
                    if (count := due(F["ag2"], t.through(4))) is not None:
                        act.wait_ge(F["ag2"], count)
                    if (count := due(F["rs2"], t.before(4))) is not None:
                        act.wait_ge(F["rs2"], count)
                    act.activation(small(SD2), f_mv[:, 2, :, 1], ACT.Sqrt, bias=eps_col[:, 0:1]).then_inc(F["sd2"], 1)
                if c := t.at(2):
                    if (count := due(F["TB"], t.through(2))) is not None:
                        act.wait_ge(F["TB"], count)
                    if (count := due(F["m1"], t.through(3))) is not None:
                        act.wait_ge(F["m1"], count)
                    if (count := due(F["scan"], t.through(3))) is not None:
                        act.wait_ge(F["scan"], count)
                    act.activation(cols(f_zBT), bank[2][:, :], ACT.Copy).then_inc(F["zBT"], 1)
                if c := t.at(5):
                    if (count := due(F["mr"], t.through(5))) is not None:
                        act.wait_ge(F["mr"], count)
                    if (count := due(F["sd3"], t.through(6))) is not None:
                        act.wait_ge(F["sd3"], count)
                    for j in range(TILES):
                        last = act.activation(junk[:, j, :], bank[7][:, j * P:(j + 1) * P], ACT.Square,
                                              accum_out=small(SS)[:, j:j + 1])
                    last.then_inc(F["sq"], 1)
                    if (count := due(F["sq"], t.through(5))) is not None:
                        act.wait_ge(F["sq"], count)
                    if (count := due(F["nm"], t.through(6))) is not None:
                        act.wait_ge(F["nm"], count)
                    act.activation(small(SD3), small(SS), ACT.Sqrt).then_inc(F["sd3"], 1)
            pipeline(act, EG, FIRST_LAG, step)

        def transposes(pe, to, rows, done):
            for j in range(TILES):
                last = pe.transpose(to[:, j * P:(j + 1) * P], rows[:, j, :], ident[:, :])
            last.then_inc(done, 1)

        def rows_matmul(pe, to, columns, w, bias, done):
            if bias is not None:
                pe.matmul(to[:, :], ones3[:, :],
                          bias3[:, ROW_BIASES.index(bias), :, :].rearrange("k j d -> k (j d)"),
                          start=True, stop=False)
            for j in range(TILES):
                last = pe.matmul(to[:, j * P:(j + 1) * P], columns[:, j * P:(j + 1) * P], w_sb[w][:, :],
                                 start=bias is None, stop=bias is None or j == TILES - 1)
            last.then_inc(done, 1)

        def first_pe(pe):
            def step(t):
                if c := t.at(3):
                    if (count := due(F["zBT"], t.through(3))) is not None:
                        pe.wait_ge(F["zBT"], count)
                    if (count := due(F["x2e"], t.before(4))) is not None:
                        pe.wait_ge(F["x2e"], count)
                    pe.matmul(bank[0][:, :], w_sb["gcn1"][:, :], cols(f_zBT), start=True, stop=True).then_inc(F["m1"], 1)
                if c := t.at(4):
                    if (count := due(F["z1"], t.through(4))) is not None:
                        pe.wait_ge(F["z1"], count)
                    if (count := due(F["xx"], t.before(4))) is not None:
                        pe.wait_ge(F["xx"], count)
                    transposes(pe, bank[1], z1_ring[:, c.s, :, :], F["Tz1"])
                if c := t.at(5):
                    if (count := due(F["y2"], t.through(5))) is not None:
                        pe.wait_ge(F["y2"], count)
                    if (count := due(F["feat"], t.before(5))) is not None:
                        pe.wait_ge(F["feat"], count)
                    transposes(pe, bank[4], f_y2, F["Tg"])
                if c := t.at(4):
                    if (count := due(F["x2T"], t.through(4))) is not None:
                        pe.wait_ge(F["x2T"], count)
                    if (count := due(F["x1T"], t.through(3))) is not None:
                        pe.wait_ge(F["x1T"], count)
                    transposes(pe, bank[0], f_x2T, F["Tx2"])
                if c := t.at(3):
                    if (count := due(F["x1T"], t.through(3))) is not None:
                        pe.wait_ge(F["x1T"], count)
                    transposes(pe, bank[2], f_x1T, F["Tx1"])
                    if (count := due(F["x2T"], t.through(4))) is not None:
                        pe.wait_ge(F["x2T"], count)
                    pe.matmul(bank[3][:, :], w_sb["gcn2"][:, :], cols(f_x1T), start=True, stop=True).then_inc(F["m2"], 1)
                    if (count := due(F["U"], t.through(3))) is not None:
                        pe.wait_ge(F["U"], count)
                    rows_matmul(pe, bank[5], cols(f_U), "gcn1", None, F["mU"])
                if c := t.at(4):
                    if (count := due(F["z1T"], t.through(4))) is not None:
                        pe.wait_ge(F["z1T"], count)
                    rows_matmul(pe, bank[1], cols(f_x2T), "gcn3", "gcn3", F["m3"])
                    if (count := due(F["R"], t.before(4))) is not None:
                        pe.wait_ge(F["R"], count)
                    rows_matmul(pe, bank[6], cols(f_z1T), "gcn2", None, F["mR"])
                if c := t.at(5):
                    if (count := due(F["gT"], t.through(5))) is not None:
                        pe.wait_ge(F["gT"], count)
                    rows_matmul(pe, bank[4], cols(f_gT), "pool", "pool", F["mf"])
                    if (count := due(F["h"], t.through(6))) is not None:
                        pe.wait_ge(F["h"], count)
                    rows_matmul(pe, bank[7], cols(f_gT), "self1", "one", F["mr"])
                if c := t.at(2):
                    if (count := due(F["nA"], t.through(2))) is not None:
                        pe.wait_ge(F["nA"], count)
                    if (count := due(F["v"], t.through(3))) is not None:
                        pe.wait_ge(F["v"], count)
                    transposes(pe, bank[5], f_zA, F["TA"])
                    if (count := due(F["nB"], t.through(2))) is not None:
                        pe.wait_ge(F["nB"], count)
                    if (count := due(F["x1e"], t.through(3))) is not None:
                        pe.wait_ge(F["x1e"], count)
                    transposes(pe, bank[2], f_zB, F["TB"])
            pipeline(pe, EG, FIRST_LAG, step)

        g_ring, self_ring, more_ring, msg_ring, self_out_ring, xx_out_ring = ring[0:6]
        d_w, d_S0, d_S1, d_v, d_n, d_nT = buf[0:6]
        d_S = (d_S0, d_S1)
        STAGES = {
            1: "staged numbers TB scan mU v msg Tg gT mf fin",
            2: "staged numbers TB scan mU v xx bn ag sd s1 tb y2 Tg gT mf mr msg fin",
            3: "staged numbers w TB scan mU v sq sd nm s1 msg Tg gT mf fin",
            4: "staged numbers w TB scan mU v fin",
        }
        RINGS = {1: "gathered seg self out1 out2", 2: "gathered seg self more out1 out2 out3",
                 3: "gathered seg self out1 out2", 4: "gathered seg self more scattered"}
        D = {k: stage(k) for k in dict.fromkeys(" ".join(STAGES.values()).split())}
        DR = {"gathered": f_xs_in, "seg": f_seg_in, "self": ring_sems("r_in"), "more": ring_sems("more_in"),
              "out1": f_z1_out, "out2": f_r_out, "out3": f_xd_out, "scattered": t_scattered}
        TAKES = {1: "gcn2", 2: "gcn3", 3: "neigh1", 4: "neigh2"}
        SCALE = {1: DINV, 2: DINV, 3: CINV, 4: CD}

        EDGES = Part(EG, 6)

        def dmas_due(name, c, more=0):
            each = 16 * TILES if name in ("gathered", "scattered") else 16
            return due(DR[name][c.s], (c.r + more) * each)

        def product_lag(k):
            return 4 if k == 1 else 5

        def round_sp(sp, k):

            def load(c, name, to, from_):
                sp.dma_start(to[:, c.s, :, :], edge_rows(from_, c)).then_inc(DR[name][c.s], 16)

            def store(c, name, to, from_):
                sp.dma_start(edge_rows(to, c), from_[:, c.s, :, :]).then_inc(DR[name][c.s], 16)

            def step(t):
                if c := t.at(1):
                    if (count := due(D["scan"], t.through(1) - RING)) is not None:
                        sp.wait_ge(D["scan"], count)
                    load_segments(sp, c, 1 if k == 3 else 0, DR["seg"])
                    if (count := due(D["v"], t.through(1) - RING)) is not None:
                        sp.wait_ge(D["v"], count)
                    load(c, "self", self_ring, self_rows[(k + 1) % 2])
                    if k in (2, 4):
                        if (count := due(D["xx" if k == 2 else "fin"], t.through(1) - RING)) is not None:
                            sp.wait_ge(D["xx" if k == 2 else "fin"], count)
                        load(c, "more", more_ring, x_dst if k == 2 else xx_dst)
                if k == 2 and (c := t.at(5)):
                    if (count := due(D["y2"], t.through(5))) is not None:
                        sp.wait_ge(D["y2"], count)
                    store(c, "out3", xx_dst, xx_out_ring)
                if k in (1, 3) and (c := t.at(5)):
                    if (count := due(D["msg"], t.through(5))) is not None:
                        sp.wait_ge(D["msg"], count)
                    store(c, "out1", table[k + 1], msg_ring)
                if k < 4 and (c := t.at(6)):
                    if k == 2:
                        if (count := due(D["msg"], t.through(6))) is not None:
                            sp.wait_ge(D["msg"], count)
                        store(c, "out1", table[k + 1], msg_ring)
                    if (count := due(D["fin"], t.through(6))) is not None:
                        sp.wait_ge(D["fin"], count)
                    store(c, "out2", self_rows[k % 2], self_out_ring)
            return [(EDGES, step)]

        def round_stored(sp, k):
            for name in ("out1", "out2", "out3"):
                if name in RINGS[k].split():
                    for s in range(RING):
                        sp.wait_ge(DR[name][s], dmas_due(name, Turn(s, uses(EG, s), s)))

        def round_pool(pool, k):
            table_limit = Limit(pool, table[k])
            out_limit = Limit(pool, out)

            def step(t):
                if k == 4 and (c := t.at(4)):
                    if (count := due(D["fin"], t.through(4))) is not None:
                        pool.wait_ge(D["fin"], count)
                    out_limit.set()
                    for j in range(TILES):
                        pool.indirect_dma_start(
                            out=out, out_offset=bass.IndirectOffsetOnAxis(ap=st_i[:, c.s, j, SCAT:SCAT + 1], axis=0),
                            in_=self_out_ring[:, c.s, j, :], in_offset=None, bounds_check=out_limit.register,
                            oob_is_err=False).then_inc(DR["scattered"][c.s], 16)
                if c := t.at(1):
                    if (count := due(D["staged"], t.through(1))) is not None:
                        pool.wait_ge(D["staged"], count)
                    if (count := due(D["w" if k >= 3 else "TB"], t.through(1) - RING)) is not None:
                        pool.wait_ge(D["w" if k >= 3 else "TB"], count)
                    gathers(pool, c, g_ring, table[k], table_limit, TAB, DR["gathered"])
            return [(EDGES, step)]

        D_SD, D_RS, D_TB, D_SS, D_NM = range(5)

        def round_dve(dve, k):

            def scaled(c, to, from_bank, factor, plus):
                for j in range(TILES):
                    last = dve.scalar_tensor_tensor(out=to[:, j, :], in0=bank[from_bank][:, j * P:(j + 1) * P],
                                                    scalar=st_f[:, c.s, j, factor:factor + 1], in1=plus(j),
                                                    op0=ALU.mult, op1=ALU.add)
                return last

            def indices(t):
                if c := t.at(0):
                    if (count := dmas_due("gathered", c)) is not None:
                        dve.wait_ge(DR["gathered"][c.s], count)
                    if k == 4:
                        if (count := dmas_due("scattered", c)) is not None:
                            dve.wait_ge(DR["scattered"][c.s], count)
                    dve.tensor_copy(st_i[:, c.s, :, :], group_of(edge_i, c)).then_inc(D["staged"], 1)

            def first(t):
                if k < 4:
                    indices(t)
                if k >= 3 and (c := t.at(2)):
                    if (count := due(D["numbers"], t.through(2))) is not None:
                        dve.wait_ge(D["numbers"], count)
                    if (count := dmas_due("gathered", c, 1)) is not None:
                        dve.wait_ge(DR["gathered"][c.s], count)
                    if (count := due(D["TB"], t.before(2))) is not None:
                        dve.wait_ge(D["TB"], count)
                    dve.tensor_tensor(d_w[:, :, :], g_ring[:, c.s, :, :], per_row(st_f[:, c.s, :, WEIGHT]),
                                      ALU.mult).then_inc(D["w"], 1)
                if c := t.at(3):
                    if k < 3:
                        if (count := due(D["numbers"], t.through(3))) is not None:
                            dve.wait_ge(D["numbers"], count)
                    if (count := due(D["mU"], t.through(3))) is not None:
                        dve.wait_ge(D["mU"], count)
                    if (count := dmas_due("self", c, 1)) is not None:
                        dve.wait_ge(DR["self"][c.s], count)
                    if k in (1, 3):
                        if (count := due(D["msg"], t.before(3))) is not None:
                            dve.wait_ge(D["msg"], count)
                    scaled(c, d_v, 1, SCALE[k], lambda j: self_ring[:, c.s, j, :]).then_inc(D["v"], 1)
                    if k == 2:
                        if (count := due(D["v"], t.through(3))) is not None:
                            dve.wait_ge(D["v"], count)
                        if (count := dmas_due("more", c, 1)) is not None:
                            dve.wait_ge(DR["more"][c.s], count)
                        if (count := dmas_due("out3", c)) is not None:
                            dve.wait_ge(DR["out3"][c.s], count)
                        if (count := due(D["y2"], t.through(3) - RING)) is not None:
                            dve.wait_ge(D["y2"], count)
                        dve.scalar_tensor_tensor(out=flat(xx_out_ring[:, c.s, :, :]), in0=cols(d_v), scalar=0.0,
                                                 in1=flat(more_ring[:, c.s, :, :]), op0=ALU.max,
                                                 op1=ALU.add).then_inc(D["xx"], 1)
                        if (count := due(D["xx"], t.through(3))) is not None:
                            dve.wait_ge(D["xx"], count)
                        if (count := due(D["ag"], t.before(3))) is not None:
                            dve.wait_ge(D["ag"], count)
                        for j in range(TILES):
                            last = dve.bn_stats(f_stats[:, 0, j, :], xx_out_ring[:, c.s, j, :])
                        last.then_inc(D["bn"], 1)
                    if k == 4:
                        if (count := due(D["v"], t.through(3))) is not None:
                            dve.wait_ge(D["v"], count)
                        if (count := dmas_due("more", c, 1)) is not None:
                            dve.wait_ge(DR["more"][c.s], count)
                        if (count := dmas_due("scattered", c)) is not None:
                            dve.wait_ge(DR["scattered"][c.s], count)
                        dve.scalar_tensor_tensor(out=flat(self_out_ring[:, c.s, :, :]), in0=cols(d_v), scalar=0.0,
                                                 in1=flat(more_ring[:, c.s, :, :]), op0=ALU.max,
                                                 op1=ALU.add).then_inc(D["fin"], 1)

            def second(t):
                if k == 2:
                    if (count := due(D["bn"], t.through(3))) is not None:
                        dve.wait_ge(D["bn"], count)
                    if (count := due(D["sd"], t.before(3))) is not None:
                        dve.wait_ge(D["sd"], count)
                    if (count := due(D["tb"], t.before(3))) is not None:
                        dve.wait_ge(D["tb"], count)
                if c := t.at(2):
                    if (count := due(D["TB"], t.through(2))) is not None:
                        dve.wait_ge(D["TB"], count)
                    if (count := dmas_due("seg", c, 1)) is not None:
                        dve.wait_ge(DR["seg"][c.s], count)
                    if (count := due(D["mU"], t.before(2) - 1)) is not None:
                        dve.wait_ge(D["mU"], count)
                    if (count := due(D["scan"], t.before(2))) is not None:
                        dve.wait_ge(D["scan"], count)
                    first = isinstance(c.g, int) and c.g == 0
                    start = 0.0 if first else cols(d_S[(c.s + 1) % 2])[:, ROWS - 1:ROWS]
                    ops = (ALU.add, ALU.max) if k == 3 else (ALU.mult, ALU.add)
                    dve.tensor_tensor_scan(cols(d_S[c.s % 2]), seg_ring[:, c.s, :], bank[0][:, :], start, *ops)\
                       .then_inc(D["scan"], 1)
                if k == 2 and (c := t.at(3)):
                    for j in range(TILES):
                        last = dve.bn_aggr(f_mv[:, 0, j, :], f_stats[:, 0, j, :])
                    last.then_inc(D["ag"], 1)

            def third(t):
                if k == 1 and (c := t.at(4)):
                    if (count := due(D["mf"], t.through(4))) is not None:
                        dve.wait_ge(D["mf"], count)
                    if (count := dmas_due("out2", c)) is not None:
                        dve.wait_ge(DR["out2"][c.s], count)
                    plus = bias_bc["gcn3"]
                    scaled(c, self_out_ring[:, c.s, :, :], 3, DINV, lambda j: plus[:, :]).then_inc(D["fin"], 1)
                if k == 2 and (c := t.at(3)):
                    if (count := due(D["sd"], t.through(3))) is not None:
                        dve.wait_ge(D["sd"], count)
                    if (count := due(D["y2"], t.before(3))) is not None:
                        dve.wait_ge(D["y2"], count)
                    dve.reciprocal(f_small[:, D_RS, :], f_small[:, D_SD, :]).then_inc(D["s1"], 1)
                    if (count := due(D["s1"], t.through(3))) is not None:
                        dve.wait_ge(D["s1"], count)
                    dve.scalar_tensor_tensor(out=f_small[:, D_TB, :], in0=f_mv[:, 0, :, 0], scalar=-1.0,
                                             in1=f_small[:, D_RS, :], op0=ALU.mult, op1=ALU.mult).then_inc(D["tb"], 1)
                if k == 3 and (c := t.at(3)):
                    if (count := due(D["sd"], t.through(3))) is not None:
                        dve.wait_ge(D["sd"], count)
                    dve.tensor_scalar(f_small[:, D_NM, :], f_small[:, D_SD, :], NORM_EPS, None, ALU.max)\
                       .then_inc(D["nm"], 1)
                    if (count := due(D["nm"], t.through(3))) is not None:
                        dve.wait_ge(D["nm"], count)
                    dve.reciprocal(f_small[:, D_RS, :], f_small[:, D_NM, :]).then_inc(D["s1"], 1)
                if c := t.at(0):
                    for user in {1: ("v", "msg", "fin"), 2: ("v",), 3: ("w", "v"), 4: ("w", "v")}[k]:
                        if (count := due(D[user], t.through(0) - RING)) is not None:
                            dve.wait_ge(D[user], count)
                    dve.tensor_copy(st_f[:, c.s, :, :], group_of(edge_f, c)).then_inc(D["numbers"], 1)
                if k == 4:
                    indices(t)
            return [(EDGES, first), (EDGES, second), (EDGES, third)]

        def round_act(act, k):

            def first(t):
                if k == 2 and (c := t.at(4)):
                    if (count := due(D["tb"], t.through(4))) is not None:
                        act.wait_ge(D["tb"], count)
                    if (count := due(D["Tg"], t.before(4))) is not None:
                        act.wait_ge(D["Tg"], count)
                    for j in range(TILES):
                        last = act.activation(d_n[:, j, :], xx_out_ring[:, c.s, j, :], ACT.Relu,
                                              scale=f_small[:, D_RS, j:j + 1], bias=f_small[:, D_TB, j:j + 1])
                    last.then_inc(D["y2"], 1)
                if k == 3 and (c := t.at(4)):
                    if (count := due(D["s1"], t.through(4))) is not None:
                        act.wait_ge(D["s1"], count)
                    if (count := dmas_due("out1", c)) is not None:
                        act.wait_ge(DR["out1"][c.s], count)
                    if (count := due(D["Tg"], t.through(4) - RING)) is not None:
                        act.wait_ge(D["Tg"], count)
                    for j in range(TILES):
                        last = act.activation(msg_ring[:, c.s, j, :], d_v[:, j, :], ACT.Relu,
                                              scale=f_small[:, D_RS, j:j + 1])
                    last.then_inc(D["msg"], 1)
                if k == 2 and (c := t.at(5)):
                    if (count := due(D["mf"], t.through(5))) is not None:
                        act.wait_ge(D["mf"], count)
                    if (count := dmas_due("out1", c)) is not None:
                        act.wait_ge(DR["out1"][c.s], count)
                    act.activation(flat(msg_ring[:, c.s, :, :]), bank[3][:, :], ACT.Relu).then_inc(D["msg"], 1)
                    if (count := due(D["mr"], t.through(5))) is not None:
                        act.wait_ge(D["mr"], count)
                    if (count := dmas_due("out2", c)) is not None:
                        act.wait_ge(DR["out2"][c.s], count)
                    act.activation(flat(self_out_ring[:, c.s, :, :]), bank[2][:, :], ACT.Copy).then_inc(D["fin"], 1)
                if k == 3 and (c := t.at(5)):
                    if (count := due(D["mf"], t.through(5))) is not None:
                        act.wait_ge(D["mf"], count)
                    if (count := dmas_due("out2", c)) is not None:
                        act.wait_ge(DR["out2"][c.s], count)
                    act.activation(flat(self_out_ring[:, c.s, :, :]), bank[3][:, :], ACT.Copy).then_inc(D["fin"], 1)

            def second(t):
                if k < 4 and (c := t.at(4)):
                    if (count := due(D["Tg"], t.through(4))) is not None:
                        act.wait_ge(D["Tg"], count)
                    if (count := due(D["mr" if k == 2 else "mf"], t.before(4))) is not None:
                        act.wait_ge(D["mr" if k == 2 else "mf"], count)
                    act.activation(cols(d_nT), bank[2][:, :], ACT.Copy).then_inc(D["gT"], 1)
                if k == 1 and (c := t.at(3)):
                    if (count := due(D["v"], t.through(3))) is not None:
                        act.wait_ge(D["v"], count)
                    if (count := dmas_due("out1", c)) is not None:
                        act.wait_ge(DR["out1"][c.s], count)
                    if (count := due(D["Tg"], t.through(3) - RING)) is not None:
                        act.wait_ge(D["Tg"], count)
                    for j in range(TILES):
                        last = act.activation(msg_ring[:, c.s, j, :], d_v[:, j, :], ACT.Relu,
                                              scale=st_f[:, c.s, j, DINV:DINV + 1])
                    last.then_inc(D["msg"], 1)

            def third(t):
                if k == 2 and (c := t.at(3)):
                    if (count := due(D["ag"], t.through(3))) is not None:
                        act.wait_ge(D["ag"], count)
                    if (count := due(D["s1"], t.before(3))) is not None:
                        act.wait_ge(D["s1"], count)
                    act.activation(f_small[:, D_SD, :], f_mv[:, 0, :, 1], ACT.Sqrt,
                                   bias=eps_col[:, 0:1]).then_inc(D["sd"], 1)
                if k == 3 and (c := t.at(3)):
                    if (count := due(D["v"], t.through(3))) is not None:
                        act.wait_ge(D["v"], count)
                    if (count := due(D["sd"], t.before(3))) is not None:
                        act.wait_ge(D["sd"], count)
                    for j in range(TILES):
                        last = act.activation(junk[:, j, :], d_v[:, j, :], ACT.Square,
                                              accum_out=f_small[:, D_SS, j:j + 1])
                    last.then_inc(D["sq"], 1)
                    if (count := due(D["sq"], t.through(3))) is not None:
                        act.wait_ge(D["sq"], count)
                    if (count := due(D["nm"], t.before(3))) is not None:
                        act.wait_ge(D["nm"], count)
                    act.activation(f_small[:, D_SD, :], f_small[:, D_SS, :], ACT.Sqrt).then_inc(D["sd"], 1)
            return [(EDGES, first), (EDGES, second), (EDGES, third)]

        def round_pe(pe, k):

            def products(t):
                lag = product_lag(k)
                if k < 4 and (c := t.at(lag)):
                    if (count := due(D["gT"], t.through(lag))) is not None:
                        pe.wait_ge(D["gT"], count)
                    if (count := due(D["msg" if k == 2 else "fin"], t.before(lag))) is not None:
                        pe.wait_ge(D["msg" if k == 2 else "fin"], count)
                    if k == 1:
                        rows_matmul(pe, bank[3], cols(d_nT), "gcn3", None, D["mf"])
                    if k == 2:
                        rows_matmul(pe, bank[3], cols(d_nT), "pool", "pool", D["mf"])
                        rows_matmul(pe, bank[2], cols(d_nT), "self1", "one", D["mr"])
                    if k == 3:
                        rows_matmul(pe, bank[3], cols(d_nT), "self2", "two", D["mf"])

            def first(t):
                if c := t.at(3):
                    if (count := due(D["scan"], t.through(3))) is not None:
                        pe.wait_ge(D["scan"], count)
                    if (count := due(D["v"], t.before(3))) is not None:
                        pe.wait_ge(D["v"], count)
                    rows_matmul(pe, bank[1], cols(d_S[c.s % 2]), TAKES[k], None, D["mU"])

            def second(t):
                if k > 1:
                    products(t)

            def third(t):
                if c := t.at(2):
                    if k >= 3:
                        if (count := due(D["w"], t.through(2))) is not None:
                            pe.wait_ge(D["w"], count)
                    else:
                        if (count := dmas_due("gathered", c, 1)) is not None:
                            pe.wait_ge(DR["gathered"][c.s], count)
                    if (count := due(D["scan"], t.before(2))) is not None:
                        pe.wait_ge(D["scan"], count)
                    transposes(pe, bank[0], d_w if k >= 3 else g_ring[:, c.s, :, :], D["TB"])
                if k < 4 and (c := t.at(4)):
                    if (count := due(D["y2" if k == 2 else "msg"], t.through(4))) is not None:
                        pe.wait_ge(D["y2" if k == 2 else "msg"], count)
                    if (count := due(D["fin" if k == 2 else "gT"], t.before(4))) is not None:
                        pe.wait_ge(D["fin" if k == 2 else "gT"], count)
                    transposes(pe, bank[2], d_n if k == 2 else msg_ring[:, c.s, :, :], D["Tg"])

            def fourth(t):
                if k == 1:
                    products(t)
            return [(EDGES, first), (EDGES, second), (EDGES, third), (EDGES, fourth)]

        def phase(sp=None, pool=None, dve=None, act=None, pe=None):
            with nc.Block() as block:
                if sp:
                    @block.sync
                    def _(engine):
                        sp(engine)
                if pool:
                    @block.gpsimd
                    def _(engine):
                        pool(engine)
                if dve:
                    @block.vector
                    def _(engine):
                        dve(engine)
                if act:
                    @block.scalar
                    def _(engine):
                        act(engine)
                if pe:
                    @block.tensor
                    def _(engine):
                        pe(engine)

        def const_loads(sp):
            for k, name in enumerate(("gcn1", "gcn2", "one")):
                sp.dma_start(bias_col[:, k:k + 1], B[name].rearrange("(p a) -> p a", a=1)).then_inc(bias_in, 16)
            for k, name in enumerate(ROW_BIASES):
                sp.dma_start(bias_row[:, k, :], B[name].rearrange("(a n) -> a n", a=1)).then_inc(bias_in, 16)
            for k in bias_bc:
                sp.dma_start(bias_bc[k][:, :], B[k].rearrange("(a n) -> a n", a=1).broadcast_to([P, P]))\
                  .then_inc(bias_bc_in, 16)
            for k in W:
                sp.dma_start(w_sb[k][:, :], W[k]).then_inc(w_in, 16)

        def bias_parts(sp):
            sp.wait_ge(bias_split, BIAS_SPLIT_ALL)
            for k in range(3):
                for j in range(TILES):
                    sp.dma_start(bias3[k:k + 1, :, j, :], bias_part[k][:, :, :]).then_inc(bias3_in, 16)

        def const_arrived(sp):
            sp.wait_ge(bias_in, 16 * (3 + len(ROW_BIASES)))
            sp.wait_ge(bias_bc_in, 16 * len(bias_bc))
            sp.wait_ge(w_in, 16 * len(W))
            sp.wait_ge(bias3_in, 16 * 3 * TILES)

        def const_pool(pool):
            pool.memset(ones3[:, :], 1.0).then_inc(ones3_done, 1)
            pool.memset(ones_col[:, :], 1.0).then_inc(ones_col_done, 1)
            pool.memset(ident[:, :], 0.0).then_inc(zeros_done, 1)
            pool.wait_ge(zeros_done, 1)
            pool.affine_select(out=ident[:, :], in_=ident[:, :], compare_op=ALU.not_equal, fill=1.0, base=0,
                               pattern=[[-1, P]], channel_multiplier=1).then_inc(ident_done, 1)

        ONE, FOUR = 16, 16 * TILES

        def prep_phase_sp(sp):
            const_loads(sp)
            zero_dmas = prep_loads(sp)
            prep_carries(sp, zero_dmas)
            bias_parts(sp)
            const_arrived(sp)

        def prep_phase_pool(pool):
            prep_pool(pool)
            const_pool(pool)

        def prep_phase_dve(dve):
            const_dve(dve)
            prep_dve(dve)

        phase(prep_phase_sp, prep_phase_pool, prep_phase_dve, prep_act, prep_pe)

        TABLE = Part(EG, 1)
        TABLE_QUADS, ROUND_QUADS = (-(-(EG + lag) // RING) for lag in (TABLE.last_lag, EDGES.last_lag))
        NODES_BEFORE = TABLE_QUADS * RING - 8
        early = Nodes(0, NODES_BEFORE, dve_norm=True)

        def table_phase_sp(sp):
            run(sp, TABLE_QUADS, node_sp(sp, early))
            node_stored(sp, NODES_BEFORE)

        def table_phase_pool(pool):
            run(pool, TABLE_QUADS, [(TABLE, table_pool(pool)), *node_pool(pool, early)])
            table_scattered(pool)

        phase(table_phase_sp, table_phase_pool,
              lambda dve: run(dve, TABLE_QUADS, [(TABLE, table_dve(dve)), *node_dve(dve, early)]),
              lambda act: run(act, TABLE_QUADS, node_act(act, early)),
              lambda pe: run(pe, TABLE_QUADS, node_pe(pe, early)))
        passed(EG, ["staged"], {"scattered": FOUR})
        passed(NODES_BEFORE, NODE_STAGES.values(), {"loaded": ONE, "stored": ONE})

        phase(first_sp, first_pool, first_dve, first_act, first_pe)
        passed(EG, F, {"pg_in": FOUR, "xs_in": FOUR, "xd_in": FOUR, "seg_in": ONE, "xd_out": ONE, "z1_out": ONE,
                       "r_out": ONE, **{f"t{k}_out": ONE for k in (1, 2, 3, 4)}})

        IN_RINGS = {"gathered": ("xs_in", FOUR), "seg": ("seg_in", ONE), "self": ("r_in", ONE), "more": ("more_in", ONE),
                    "out1": ("z1_out", ONE), "out2": ("r_out", ONE), "out3": ("xd_out", ONE)}
        NODES_AFTER = NG - NODES_BEFORE
        assert 3 * ROUND_QUADS * RING >= NODES_AFTER + 8

        def merged(a, b):
            both = []
            for i in range(max(len(a), len(b))):
                both += a[i:i + 1] + b[i:i + 1]
            return both

        def rounds(k):
            late = Nodes(NODES_BEFORE, NODES_AFTER, (k - 1) * ROUND_QUADS)

            def sp(engine):
                run(engine, ROUND_QUADS, round_sp(engine, k) + node_sp(engine, late))
                round_stored(engine, k)
                if k == 3:
                    node_stored(engine, NODES_AFTER)

            def pool(engine):
                run(engine, ROUND_QUADS, round_pool(engine, k) + node_pool(engine, late))

            def dve(engine):
                run(engine, ROUND_QUADS, merged(node_dve(engine, late), round_dve(engine, k)))

            def act(engine):
                run(engine, ROUND_QUADS, merged(node_act(engine, late), round_act(engine, k)))

            def pe(engine):
                run(engine, ROUND_QUADS, merged(node_pe(engine, late), round_pe(engine, k)))

            phase(sp, pool, dve, act, pe)

        for k in (1, 2, 3):
            rounds(k)
            passed(EG, STAGES[k].split(), dict(IN_RINGS[name] for name in RINGS[k].split()))

        def last_pool(pool):
            run(pool, ROUND_QUADS, round_pool(pool, 4))
            for s in range(RING):
                pool.wait_ge(DR["scattered"][s], dmas_due("scattered", Turn(s, uses(EG, s), s)))

        phase(lambda sp: run(sp, ROUND_QUADS, round_sp(sp, 4)), last_pool,
              lambda dve: run(dve, ROUND_QUADS, round_dve(dve, 4)), None,
              lambda pe: run(pe, ROUND_QUADS, round_pe(pe, 4)))


_W = {"gcn1": "L0_gnn_W1", "gcn2": "L0_gnn_W2", "gcn3": "L0_gnn_W3", "pool": "L1_gnn_W_pool",
      "self1": "L1_gnn_W1_self", "neigh1": "L1_gnn_W1_neigh", "self2": "L1_gnn_W2_self", "neigh2": "L1_gnn_W2_neigh"}
_B = {"gcn1": "L0_gnn_b1", "gcn2": "L0_gnn_b2", "gcn3": "L0_gnn_b3", "pool": "L1_gnn_b_pool",
      "one": "L1_gnn_b1", "two": "L1_gnn_b2"}


def kernel(**inputs):
    import numpy as _np
    import concourse.bacc as _bacc
    from concourse.bass_utils import run_bass_kernel_spmd as _run

    nc = _bacc.Bacc("TRN2", target_bir_lowering=False, num_devices=1)
    arrays, aps = {}, {}
    for name in ["x", "src", "dst", "edge_weight", *_W.values(), *_B.values()]:
        a = _np.ascontiguousarray(inputs[name])
        arrays[name] = a
        aps[name] = nc.dram_tensor(name, a.shape, mybir.dt.from_np(a.dtype), kind="ExternalInput").ap()
    out = nc.dram_tensor("out", inputs["x"].shape, F32, kind="ExternalOutput").ap()
    gnn_kernel(nc, aps["x"], aps["src"], aps["dst"], aps["edge_weight"],
               {k: aps[v] for k, v in _W.items()}, {k: aps[v] for k, v in _B.items()}, out)
    r = _run(nc, [arrays], core_ids=[0])
    return r.results[0]["out"]
```
